# Optimizing a Trainium2 kernel written in Bass

```python
import numpy as np
import jax
import jax.numpy as jnp

def _softmax(x, axis=-1):
    return jax.nn.softmax(x, axis=axis)

def _gelu(x):
    return jax.nn.gelu(x, approximate=True)

def _silu(x):
    return jax.nn.silu(x)

def _sigmoid(x):
    return jax.nn.sigmoid(x)

def _layernorm(x, axis=-1, eps=1e-05):
    m = jnp.mean(x, axis=axis, keepdims=True)
    v = jnp.var(x, axis=axis, keepdims=True)
    return (x - m) / jnp.sqrt(v + eps)

def _scatter_add(tgt, idx, src, axis=0):
    return tgt.at[idx].add(src)

def _segment_sum(src, seg, n):
    return jax.ops.segment_sum(src, seg, n)
kernel_name = 'mk_gnn_resnorm_d4_gnn_r16_0c8bf1'

def setup_inputs(seed: int=0):
    np.random.seed(seed)
    _w = jnp.asarray

    def _rec_inputs():
        import jax
        import jax.numpy as jnp
        _gk = jax.random.key(seed)
        x = -0.0003713 + 1 * jax.random.normal(jax.random.fold_in(_gk, 1), (6250, 256), jnp.float32)
        _s = jax.random.randint(jax.random.fold_in(_gk, 2), (50000,), 0, 6250, jnp.int32)
        _d = jax.random.randint(jax.random.fold_in(_gk, 3), (50000,), 0, 6250, jnp.int32)
        _loop = jnp.arange(6250, dtype=jnp.int32)
        src = jnp.concatenate([_s, _d, _loop])
        dst = jnp.concatenate([_d, _s, _loop])
        _o = jnp.argsort(dst, stable=True)
        src = src[_o]
        dst = dst[_o]
        edge_weight = jax.random.uniform(jax.random.fold_in(_gk, 12), (106250,), jnp.float32, 0.0, 0.999999)
        return (x, src, dst, edge_weight)
    x, src, dst, edge_weight = _rec_inputs()

    def _L0_gnn_setup():
        import jax, jax.numpy as jnp
        import numpy as np
        N, IN_CH, HEADS, OUT_CH, E = (3125, 256, 4, 64, 50000)
        key = jax.random.key(seed)
        k1, k2, k3, k4, k5 = jax.random.split(key, 5)
        x = jax.random.normal(k1, (N, IN_CH), dtype=jnp.float32)
        edge_index = jax.random.randint(k2, (2, E), 0, N, dtype=jnp.int64)
        bw = float(np.sqrt(6.0 / (IN_CH + HEADS * OUT_CH)))
        ba = float(np.sqrt(6.0 / (HEADS + OUT_CH)))
        weight = jax.random.uniform(k3, (IN_CH, HEADS * OUT_CH), jnp.float32, -bw, bw)
        attn_l = jax.random.uniform(k4, (HEADS, OUT_CH), jnp.float32, -ba, ba)
        attn_r = jax.random.uniform(k5, (HEADS, OUT_CH), jnp.float32, -ba, ba)
        return {'x': x, 'edge_index': edge_index, 'weight': weight, 'attn_l': attn_l, 'attn_r': attn_r}
    _L0_gnn_all = _L0_gnn_setup()
    _L0_gnn_in = {k: v for k, v in _L0_gnn_all.items() if k in ('weight', 'attn_l', 'attn_r')}
    del _L0_gnn_all

    def _L1_gnn_setup():
        import jax, jax.numpy as jnp
        import numpy as np
        N_NODES = 3125
        key = jax.random.key(seed)
        k1, k2, k3 = jax.random.split(key, 3)
        x = jax.random.normal(k1, (N_NODES, 256), dtype=jnp.float32)
        W = jax.random.normal(k2, (256, 256), dtype=jnp.float32) * (1.0 / np.sqrt(256))
        edge_index = jax.random.randint(k3, (2, 100000), 0, N_NODES, dtype=jnp.int64)
        return {'x': x, 'W': W, 'edge_index': edge_index}
    _L1_gnn_all = _L1_gnn_setup()
    _L1_gnn_in = {k: v for k, v in _L1_gnn_all.items() if k in ('W',)}
    del _L1_gnn_all

    def _L2_gnn_setup():
        import jax, jax.numpy as jnp
        import numpy as np
        N_NODES = 3125
        N_EDGES = 100000
        D = 256

        def gcn_layer(x, row, col, w, W, b, n):
            x = x @ W
            deg = jax.ops.segment_sum(w, col, num_segments=n)
            dinv = jnp.where(deg > 0, jax.lax.rsqrt(deg), jnp.zeros((), x.dtype))
            norm = dinv[row] * w * dinv[col]
            out = jax.ops.segment_sum(norm[:, None] * x[row], col, num_segments=n)
            return out + b
        key = jax.random.key(seed)
        ks = jax.random.split(key, 6)
        X = jax.random.normal(ks[0], (N_NODES, D), dtype=jnp.float32)
        edge_index = jax.random.randint(ks[1], (2, N_EDGES), 0, N_NODES, dtype=jnp.int64)
        edge_weight = jax.random.uniform(ks[2], (N_EDGES,), dtype=jnp.float32)
        scale = 1.0 / np.sqrt(D)
        W1 = jax.random.normal(ks[3], (D, D), dtype=jnp.float32) * scale
        b1 = jnp.zeros((D,), dtype=jnp.float32)
        W2 = jax.random.normal(ks[4], (D, D), dtype=jnp.float32) * scale
        b2 = jnp.zeros((D,), dtype=jnp.float32)
        return {'X': X, 'edge_index': edge_index, 'edge_weight': edge_weight, 'W1': W1, 'b1': b1, 'W2': W2, 'b2': b2}
    _L2_gnn_all = _L2_gnn_setup()
    _L2_gnn_in = {k: v for k, v in _L2_gnn_all.items() if k in ('W1', 'b1', 'W2', 'b2')}
    del _L2_gnn_all

    def _L3_gnn_setup():
        import jax, jax.numpy as jnp
        import numpy as np
        key = jax.random.key(seed)
        k1, k2, k3 = jax.random.split(key, 3)
        N, E, D_IN, D_OUT = (6250, 200000, 256, 256)
        x = jax.random.normal(k1, (N, D_IN), dtype=jnp.float32)
        W = jax.random.normal(k2, (D_OUT, D_IN), dtype=jnp.float32) * (1.0 / np.sqrt(D_IN))
        edge_index = jax.random.randint(k3, (2, E), 0, N, dtype=jnp.int32)
        return {'x': x, 'W': W, 'edge_index': edge_index}
    _L3_gnn_all = _L3_gnn_setup()
    _L3_gnn_in = {k: v for k, v in _L3_gnn_all.items() if k in ('W',)}
    del _L3_gnn_all
    return {'x': x, 'src': src, 'dst': dst, 'edge_weight': edge_weight, 'L0_gnn_weight': _L0_gnn_in['weight'], 'L0_gnn_attn_l': _L0_gnn_in['attn_l'], 'L0_gnn_attn_r': _L0_gnn_in['attn_r'], 'L1_gnn_W': _L1_gnn_in['W'], 'L2_gnn_W1': _L2_gnn_in['W1'], 'L2_gnn_b1': _L2_gnn_in['b1'], 'L2_gnn_W2': _L2_gnn_in['W2'], 'L2_gnn_b2': _L2_gnn_in['b2'], 'L3_gnn_W': _L3_gnn_in['W']}

def reference(x, src, dst, edge_weight, L0_gnn_weight, L0_gnn_attn_l, L0_gnn_attn_r, L1_gnn_W, L2_gnn_W1, L2_gnn_b1, L2_gnn_W2, L2_gnn_b2, L3_gnn_W):
    import jax
    import jax.numpy as jnp

    def _L0_gnn_ref(x, edge_index, weight, attn_l, attn_r):
        import jax, jax.numpy as jnp
        import numpy as np
        N, IN_CH, HEADS, OUT_CH, E = (3125, 256, 4, 64, 50000)
        heads, out_ch = attn_l.shape
        n = x.shape[0]
        xt = jnp.matmul(x, weight).reshape(-1, heads, out_ch)
        row, col = (edge_index[0], edge_index[1])
        alpha_l = jnp.einsum('ehd,hd->eh', xt[row], attn_l)
        alpha_r = jnp.einsum('ehd,hd->eh', xt[col], attn_r)
        alpha = jax.nn.softmax(jax.nn.leaky_relu(alpha_l + alpha_r, 0.01), axis=1)
        tmp = jnp.einsum('nh,nhd->nd', alpha[:n], xt[col[:n]])
        out = jnp.broadcast_to(tmp[:, None, :], (n, heads, out_ch))
        return out.reshape(n, heads * out_ch)

    def _L1_gnn_ref(x, W, edge_index):
        import jax, jax.numpy as jnp
        import numpy as np
        N_NODES = 3125
        N = x.shape[0]
        src, dst = (edge_index[0], edge_index[1])
        h = x @ W
        deg = jax.ops.segment_sum(jnp.ones_like(dst, dtype=h.dtype), dst, num_segments=N)
        deg_inv_sqrt = jnp.where(deg > 0, jax.lax.rsqrt(jnp.maximum(deg, 1)), 0.0)
        norm = deg_inv_sqrt[src] * deg_inv_sqrt[dst]
        msgs = h[src] * norm[:, None]
        out = jax.ops.segment_sum(msgs, dst, num_segments=N)
        return out

    def _L2_gnn_ref(X, edge_index, edge_weight, W1, b1, W2, b2):
        import jax, jax.numpy as jnp
        import numpy as np
        N_NODES = 3125
        N_EDGES = 100000
        D = 256

        def gcn_layer(x, row, col, w, W, b, n):
            x = x @ W
            deg = jax.ops.segment_sum(w, col, num_segments=n)
            dinv = jnp.where(deg > 0, jax.lax.rsqrt(deg), jnp.zeros((), x.dtype))
            norm = dinv[row] * w * dinv[col]
            out = jax.ops.segment_sum(norm[:, None] * x[row], col, num_segments=n)
            return out + b
        n = X.shape[0]
        loop = jnp.arange(n, dtype=edge_index.dtype)
        row = jnp.concatenate([edge_index[0], loop])
        col = jnp.concatenate([edge_index[1], loop])
        w = jnp.concatenate([edge_weight, jnp.ones((n,), X.dtype)])
        h = jax.nn.relu(gcn_layer(X, row, col, w, W1, b1, n))
        h = jax.nn.relu(gcn_layer(h, row, col, w, W2, b2, n))
        return h

    def _L3_gnn_ref(x, W, edge_index):
        import jax, jax.numpy as jnp
        import numpy as np
        N = x.shape[0]
        loops = jnp.arange(N, dtype=edge_index.dtype)
        src = jnp.concatenate([edge_index[0], loops])
        dst = jnp.concatenate([edge_index[1], loops])
        deg = jax.ops.segment_sum(jnp.ones_like(src, dtype=x.dtype), src, num_segments=N)
        deg_rsqrt = jax.lax.rsqrt(deg)
        vals = deg_rsqrt[src] * deg_rsqrt[dst]
        h = x @ W.T
        msgs = vals[:, None] * h[dst]
        out = jax.ops.segment_sum(msgs, src, num_segments=N)
        return out
    edge_index = jnp.stack([src, dst])
    x = _layernorm(x + _L0_gnn_ref(x, edge_index, L0_gnn_weight, L0_gnn_attn_l, L0_gnn_attn_r), axis=-1)
    x = _layernorm(x + _L1_gnn_ref(x, L1_gnn_W, edge_index), axis=-1)
    x = _layernorm(x + _L2_gnn_ref(x, edge_index, edge_weight, L2_gnn_W1, L2_gnn_b1, L2_gnn_W2, L2_gnn_b2), axis=-1)
    x = _layernorm(x + _L3_gnn_ref(x, L3_gnn_W, edge_index), axis=-1)
    return x

_drawn_inputs = setup_inputs


def setup_inputs(seed=0):
    import zlib

    import numpy as np

    out = dict(_drawn_inputs(seed))
    spreads = {'L2_gnn_b1': (0.0, 0.1), 'L2_gnn_b2': (0.0, 0.1)}
    factors = {}
    for name, (base, spread) in spreads.items():
        noise = np.random.default_rng([zlib.crc32(name.encode()), seed]).standard_normal(out[name].shape)
        drawn = base * np.exp(spread * noise) if base else spread * noise
        out[name] = jnp.asarray(drawn.astype(out[name].dtype))
    for name, factor in factors.items():
        out[name] = (out[name] * factor).astype(out[name].dtype)
    return out
```

```python
from contextlib import ExitStack

import concourse.bass as bass
from concourse import mybir

F32 = mybir.dt.float32
BF16 = mybir.dt.bfloat16
I32 = mybir.dt.int32
U32 = mybir.dt.uint32
U16 = mybir.dt.uint16
ALU = mybir.AluOpType
ACT = mybir.ActivationFunctionType
AX = mybir.AxisListType

N, D, E = 6250, 256, 106250
P = 128
NBK = 49
LAST = N - (NBK - 1) * P
EC = 831
ETAIL = E - (P - 1) * EC
NCH = E // P + NBK + 1
NCH += -NCH % 4
AW = 264
EPS = 1e-5
NG, NM, NA = 7, 4, 4
UNSLOTTED = float(127 + 128 * 1000)


class Queues:

    def __init__(self, sems):
        self.sem = sems
        self.n = {e: 0 for e in sems}
        self.dma_n = {}
        self.seen = {e: {} for e in list(sems) + ["sync"]}
        self.code = {e: [] for e in list(sems) + ["sync"]}

    def _waits(self, eng, waits):
        out = []
        for sem, val in waits:
            if self.seen[eng].get(sem, 0) < val:
                self.seen[eng][sem] = val
                out.append((sem, val))
        return out

    def op(self, eng, fn, *waits):
        self.n[eng] += 1
        self.code[eng].append((self._waits(eng, waits), fn, self.sem[eng], 1))
        return (self.sem[eng], self.n[eng])

    def dma(self, eng, fn, sem, *waits):
        self.dma_n[sem] = self.dma_n.get(sem, 0) + 16
        self.code[eng].append((self._waits(eng, waits), fn, sem, 16))
        return (sem, self.dma_n[sem])

    def plain(self, eng, fn, *waits):
        self.code[eng].append((self._waits(eng, waits), fn, None, 0))

    def run(self, name, eng):
        for waits, fn, sem, by in self.code[name]:
            for s, v in waits:
                eng.wait_ge(s, v)
            ins = fn(eng)
            if sem is not None:
                ins.then_inc(sem, by)


def program(nc, a, out):
    dr = lambda n, s, d=F32: nc.dram_tensor(n, s, d, kind="Internal").ap()
    T0, T1, T2, T3, T4 = (dr("T0", (N, 260)), dr("T1", (N + 1, D)), dr("T2", (N + 1, D)),
                          dr("T3", (N + 1, D)), dr("T4", (N + 1, D)))
    TL = dr("TL", (N, 4))
    SLOTD, SLOTS = dr("SLOTD", (P * NCH, 2)), dr("SLOTS", (P * NCH, 1))
    BKD, BKS = dr("BKD", (1, 896), I32), dr("BKS", (1, 896), I32)
    with ExitStack() as ctx:
        sb = lambda n, s, d=F32: ctx.enter_context(nc.sbuf_tensor(n, s, d))
        sem = lambda n: ctx.enter_context(nc.semaphore(n))
        X = sb("X", [P, NBK, D])
        ACC = sb("ACC", [P, NBK, AW])
        iot = sb("iot", [P, P])
        pid = sb("pid", [P, 1])
        ident = sb("ident", [P, P])
        lower = sb("lower", [P, P])
        ones = sb("ones", [P, P])
        kio = sb("kio", [P, 7])
        W0 = sb("W0", [P, 2, AW])
        W1, W2, W3, W4r = (sb(f"Wt{i}", [P, 2, D]) for i in range(4))
        W4 = W0
        b1, b2 = (sb(f"bc{i}", [P, D]) for i in range(2))
        hb = [sb(f"hb{i}", [P, D]) for i in range(3)]
        atl, atr, wtmp = hb
        keyi = [sb(f"keyi{i}", [P, EC], I32) for i in range(2)]
        we = sb("we", [P, EC])
        hi = sb("hi", [P, EC], BF16)
        lof = sb("lof", [P, EC])
        zb = sb("zb", [P, EC], BF16)
        mm = [sb(f"mm{i}", [P, EC], BF16) for i in range(2)]
        sc = [sb(f"sc{i}", [P, EC]) for i in range(2)]
        ti, tj = (t_[:, :].bitcast(I32) for t_ in sc)
        rk = sb("rk", [P, EC])
        cnt = sb("cnt", [P, NBK])
        s49 = [sb(f"s49{i}", [P, NBK]) for i in range(5)]
        i49 = [sb(f"i49{i}", [P, NBK], I32) for i in range(2)]
        bks7 = sb("bks7", [P, 7])
        bki = sb("bki", [P, 7], I32)
        adrD = sb("adrD", [P, EC], U32)
        payD = sb("payD", [P, EC, 2])
        big = [sb(f"big{i}", [P, 8 * (P + 2 * NBK)]) for i in range(2)]
        bk7 = big[0][:, 0:7 * NBK].rearrange("p (t b) -> p t b", t=7)
        SL = sb("SL", [P, NCH, 2])
        idx = sb("idx", [P, NCH], U32)
        dlo = sb("dlo", [P, NCH])
        row = sb("row", [1, 896], I32)
        srcN = sb("srcN", [P, NBK], I32)
        dstN = sb("dstN", [P, NBK], I32)
        degI, degW, degS = sb("degI", [P, NBK]), sb("degW", [P, NBK]), sb("degS", [P, NBK])
        d1, d2, d3, dk = (sb(f"d{i}", [P, NBK]) for i in range(4))
        G = [sb(f"G{i}", [P, D]) for i in range(NG)]
        M = [sb(f"M{i}", [P, P]) for i in range(NM)]
        xT = [sb(f"xT{i}", [P, 2, P]) for i in range(2)]
        st = sb("st", [P, NBK, 6])
        mv = sb("mv", [P, NBK, 2])
        rstd, nmr = sb("rstd", [P, NBK]), sb("nmr", [P, NBK])
        rq = [sb(f"rq{i}", [P, NBK]) for i in range(3)]
        al = sb("al", [P, NBK, 4])
        alb = sb("alb", [P, NBK, 4])
        amx = sb("amx", [P, NBK])
        PA = [ctx.enter_context(nc.psum_tensor(f"PA{i}", [P, 512], F32)) for i in range(NA)]
        PT = [ctx.enter_context(nc.psum_tensor(f"PT{i}", [P, 512], F32)) for i in range(2)]
        PH = [ctx.enter_context(nc.psum_tensor(f"PH{i}", [P, 512], F32)) for i in range(2)]
        q = Queues({e: sem(f"s_{e}") for e in ("vector", "scalar", "tensor", "gpsimd")})
        op, dma = q.op, q.dma
        V, S, T, G_ = "vector", "scalar", "tensor", "gpsimd"
        s_g = [sem(f"s_g{i}") for i in range(NG)]
        s_st = [sem(f"s_st{i}") for i in range(2)]
        s_sD, s_sS, s_out, s_al = sem("s_sD"), sem("s_sS"), sem("s_out"), sem("s_al")
        ndma = [0]

        def load(dst, src, *waits, eng="sync", slow=False):
            ndma[0] += 1
            return dma(eng, lambda e: e.dma_start(dst, src, allow_slow_non_contiguous=slow), sem(f"s_ld{ndma[0]}"), *waits)

        def rsqrt(dst, src, tok):
            t = op(S, lambda e: e.activation(rq[0][:, :], src, ACT.Sqrt), tok)
            t = op(V, lambda e: e.reciprocal(rq[1][:, :], rq[0][:, :]), t)
            u = op(V, lambda e: e.tensor_tensor(rq[2][:, :], rq[1][:, :], rq[1][:, :], ALU.mult), t)
            u = op(V, lambda e: e.scalar_tensor_tensor(out=rq[0][:, :], in0=src, scalar=-0.5, in1=rq[2][:, :],
                                                       op0=ALU.mult, op1=ALU.mult), u)
            return op(V, lambda e: e.scalar_tensor_tensor(out=dst[:, :], in0=rq[0][:, :], scalar=1.5, in1=rq[1][:, :],
                                                          op0=ALU.add, op1=ALU.mult), u)

        c_iot = op(G_, lambda e: e.iota(iot[:, :], [[1, P]], base=0, channel_multiplier=0,
                                        allow_small_or_imprecise_dtypes=True))
        c_pid = op(G_, lambda e: e.iota(pid[:, :], [[1, 1]], base=0, channel_multiplier=1,
                                        allow_small_or_imprecise_dtypes=True))
        c_kio = op(G_, lambda e: e.iota(kio[:, :], [[1, 7]], base=0, channel_multiplier=7,
                                        allow_small_or_imprecise_dtypes=True))
        z_idx = op(V, lambda e: e.memset(srcN[:, NBK - 1:NBK], 0))
        z_idx = op(V, lambda e: e.memset(dstN[:, NBK - 1:NBK], 0))
        z_key = [op(V, lambda e, i=i: e.memset(keyi[i][96:128, ETAIL:EC], 8192)) for i in range(2)]
        z_we = op(V, lambda e: e.memset(we[96:128, ETAIL:EC], 0.0))
        z_x = op(V, lambda e: e.memset(X[96:128, NBK - 1, :], 0.0))

        def load_edges(dst, src, z):
            load(dst[0:112, :], src[0:112 * EC].rearrange("(p c) -> p c", c=EC), z)
            load(dst[112:127, :], src[112 * EC:127 * EC].rearrange("(p c) -> p c", c=EC), z)
            t = [(s, v) for s, v in list(q.dma_n.items())[-2:]]
            return t + [load(dst[127:128, 0:ETAIL], src[127 * EC:E].rearrange("(p c) -> p c", p=1), z)]

        l_dst = load_edges(keyi[0], a["dst"], z_key[0])
        l_x = [load(X[:, 0:48, :], a["x"][0:48 * P, :].rearrange("(b p) d -> p b d", p=P)),
               load(X[0:LAST, 48, :], a["x"][48 * P:N, :], z_x)]
        l_w0 = load(W0[:, :, 0:D], a["L0_gnn_weight"].rearrange("(t p) d -> p t d", p=P), eng=S)
        l_at = [load(t_[:, :], a[n_].rearrange("(o h) d -> o (h d)", o=1).to_broadcast([P, D]), eng=S)
                for t_, n_ in ((atl, "L0_gnn_attn_l"), (atr, "L0_gnn_attn_r"))]
        l_src = load_edges(keyi[1], a["src"], z_key[1])
        l_we = load_edges(we, a["edge_weight"], z_we)
        l_w = [load(t_[:, :, :], a[n_].rearrange("(t p) d -> p t d", p=P), eng=S)
               for t_, n_ in ((W1, "L1_gnn_W"), (W2, "L2_gnn_W1"), (W3, "L2_gnn_W2"), (W4r, "L3_gnn_W"))]
        l_b = [load(t_[:, :], a[n_].rearrange("(o d) -> o d", o=1).to_broadcast([P, D]), eng=S)
               for t_, n_ in ((b1, "L2_gnn_b1"), (b2, "L2_gnn_b2"))]
        l_nodes = []
        for t_, n_ in ((srcN, "src"), (dstN, "dst")):
            l_nodes.append(load(t_[:, 0:48], a[n_][0:48 * P].rearrange("(b p) -> p b", p=P), slow=True))
            l_nodes.append(load(t_[0:LAST, 48:49], a[n_][48 * P:N].rearrange("(p o) -> p o", o=1), z_idx, slow=True))

        c_id = op(V, lambda e: e.tensor_scalar(ident[:, :], iot[:, :], pid[:, 0:1], None, ALU.is_equal), c_pid, c_iot)
        c_lo = op(V, lambda e: e.tensor_scalar(lower[:, :], iot[:, :], pid[:, 0:1], None, ALU.is_gt))
        c_on = op(V, lambda e: e.memset(ones[:, :], 1.0))
        c_zb = op(V, lambda e: e.memset(zb[:, :], 0.0))
        z_slots = op(V, lambda e: e.memset(SL[:, :, :], 0.0))
        z_sd = load(SLOTD.rearrange("(p k) o -> p (k o)", p=P), SL[:, :, :].rearrange("p k o -> p (k o)"), z_slots)
        z_ss = load(SLOTS.rearrange("(p k) o -> p (k o)", p=P),
                    SL[:, :, :].rearrange("p k o -> p (k o)")[:, 0:NCH], z_slots)
        z_rows = [load(t_[0:1, :], SL[0:1, 0:128, :].rearrange("p k o -> p (k o)"), z_slots) for t_ in (T1, T2, T3, T4)]

        wa = []
        for t in range(2):
            for col, at in ((256, atr), (260, atl)):
                m_ = op(V, lambda e, t=t, at=at: e.tensor_tensor(wtmp[:, :], W0[:, t, 0:D], at[:, :], ALU.mult),
                        l_w0, *l_at, *wa)
                wa = [op(V, lambda e, t=t, col=col: e.tensor_reduce(
                    W0[:, t, col:col + 4], wtmp[:, :].rearrange("p (h d) -> p h d", h=4), AX.X, ALU.add), m_)]

        use = {"pt": [], "ph": [], "xt": []}

        def project(src_ap, Wt, width, ready, evac):
            n = len(use["pt"])
            pt, ph, xt = PT[n % 2], PH[n % 2], xT[n % 2]
            w_pt = [use["pt"][n - 2]] if n >= 2 else []
            op(T, lambda e: e.transpose(pt[:, 0:P], src_ap[:, 0:P], ident[:, :]), c_id, *ready, *w_pt)
            tr = op(T, lambda e: e.transpose(pt[:, P:2 * P], src_ap[:, P:2 * P], ident[:, :]))
            w_xt = [use["xt"][n - 2]] if n >= 2 else []
            cp = op(S, lambda e: e.copy(xt[:, :, :].rearrange("p t n -> p (t n)"), pt[:, 0:2 * P]), tr, *w_xt)
            use["pt"].append(cp)
            w_ph = [use["ph"][n - 2]] if n >= 2 else []
            for t in range(2):
                mt = op(T, lambda e, t=t: e.matmul(ph[:, 0:width], xt[:, t, :], Wt[:, t, 0:width],
                                                  start=t == 0, stop=t == 1), cp, *w_ph)
            use["xt"].append(mt)
            use["ph"].append(evac(ph, mt))
            return tr

        def rows_of(b):
            return LAST if b == NBK - 1 else P

        t0_tok = []
        for b in range(NBK):
            ev = {}

            def evac(ph, mt, b=b, ev=ev):
                ev["t"] = op(S, lambda e: e.copy(ACC[:, b, 0:264], ph[:, 0:264]), mt)
                return ev["t"]
            project(X[:, b, :], W0, 264, [*l_x, *wa], evac)
            r = rows_of(b)
            t0_tok.append(dma("sync", lambda e, b=b, r=r: e.dma_start(T0[b * P:b * P + r, :], ACC[0:r, b, 0:260]),
                              s_st[0], ev["t"]))
            t0_tok.append(dma("sync", lambda e, b=b, r=r: e.dma_start(TL[b * P:b * P + r, :], ACC[0:r, b, 260:264]),
                              s_st[1], ev["t"]))
        t0_done = [t0_tok[-1], t0_tok[-2]]
        g0 = []
        for b in range(NBK):
            g0.append(dma(G_, lambda e, b=b: e.indirect_dma_start(
                ACC[:, b, 0:260], None, T0, bass.IndirectOffsetOnAxis(ap=dstN[:, b:b + 1].bitcast(U32), axis=0)),
                s_g[b % 2], *t0_done, *l_nodes))
            g0.append(dma(G_, lambda e, b=b: e.indirect_dma_start(
                al[:, b, :], None, TL, bass.IndirectOffsetOnAxis(ap=srcN[:, b:b + 1].bitcast(U32), axis=0)),
                s_g[2 + b % 2], *t0_done, *l_nodes))
        g0_done = g0[-4:]

        last_pay = [None]

        def rank(key, lk, oth, lo_, adr, bkdram, pay, guard):
            t = op(V, lambda e: e.tensor_scalar(ti[:, :], key[:, :], 7, None, ALU.logical_shift_right), *lk, *guard)
            t1 = op(V, lambda e: e.tensor_copy(hi[:, :], ti[:, :]), t)
            t2 = op(V, lambda e: e.tensor_scalar(tj[:, :], key[:, :], 127, None, ALU.bitwise_and))
            t2 = op(V, lambda e: e.tensor_copy(lof[:, :], tj[:, :]), t2)
            t3 = op(V, lambda e: e.tensor_scalar(rk[:, :], oth[:, :], 1.0, 128.0, ALU.add, ALU.mult), *lo_)
            t3 = op(V, lambda e: e.tensor_tensor(pay, rk[:, :], lof[:, :], ALU.add), t3, t2)
            counts = []
            for b in range(NBK):
                w_ = [counts[b - 2]] if b >= 2 else []
                counts.append(op(V, lambda e, b=b: e.tensor_scalar(mm[b % 2][:, :], hi[:, :], float(b), 0.0, ALU.is_equal,
                                                                   ALU.add, accum_out=cnt[:, b:b + 1]), t1, *w_))
            p1 = op(T, lambda e: e.matmul(PA[0][:, 0:NBK], lower[:, :], cnt[:, :], start=True, stop=True), counts[-1], c_lo)
            p2 = op(T, lambda e: e.matmul(PA[1][:, 0:NBK], ones[:, :], cnt[:, :], start=True, stop=True), c_on)
            v = op(V, lambda e: e.tensor_scalar(i49[0][:, :], PA[1][:, 0:NBK], 127.0, None, ALU.add), p2)
            v = op(V, lambda e: e.tensor_scalar(i49[1][:, :], i49[0][:, :], 7, None, ALU.logical_shift_right), v)
            v = op(V, lambda e: e.tensor_copy(s49[0][:, :], i49[1][:, :]), v)
            incl = op(V, lambda e: e.tensor_tensor_scan(s49[1][:, :], s49[0][:, :], zb[:, 0:NBK], 0.0, ALU.add, ALU.add), v, c_zb)
            v = op(V, lambda e: e.tensor_tensor(s49[2][:, :], s49[1][:, :], s49[0][:, :], ALU.subtract), incl)
            v = op(V, lambda e: e.tensor_scalar(s49[3][:, :], s49[2][:, :], 128.0, -1.0, ALU.mult, ALU.add), v)
            base = op(V, lambda e: e.tensor_tensor(s49[4][:, :], PA[0][:, 0:NBK], s49[3][:, :], ALU.add), v, p1)
            u = op(V, lambda e: e.tensor_tensor(
                bk7[:, :, :], s49[1][:, :].unsqueeze(1).to_broadcast([P, 7, NBK]),
                kio[:, :].unsqueeze(2).to_broadcast([P, 7, NBK]), ALU.is_le), incl, c_kio)
            u = op(V, lambda e: e.tensor_reduce(bks7[:, :], bk7[:, :, :], AX.X, ALU.add), u)
            u = op(V, lambda e: e.tensor_scalar(bki[:, :], bks7[:, :], float(NBK - 1), float(AW), ALU.min, ALU.mult), u)
            bk = load(bkdram.rearrange("o (p t) -> (o p) t", t=7), bki[:, :], u)
            r0 = op(V, lambda e: e.memset(rk[:, :], UNSLOTTED), t3)
            prev = []
            for b in range(NBK):
                m_ = op(V, lambda e, b=b: e.tensor_scalar(mm[b % 2][:, :], hi[:, :], float(b), None, ALU.is_equal),
                        counts[-1], *prev[-2:-1])
                s_ = op(V, lambda e, b=b: e.tensor_tensor_scan(sc[b % 2][:, :], mm[b % 2][:, :], zb[:, :],
                                                              s49[4][:, b:b + 1], ALU.add, ALU.add), m_, base, t1, t2)
                prev.append(op(V, lambda e, b=b: e.copy_predicated(rk[:, :], mm[b % 2][:, :].bitcast(U16), sc[b % 2][:, :]),
                               s_, r0, *prev[-1:]))
            v = op(V, lambda e: e.tensor_copy(ti[:, :], rk[:, :]), prev[-1])
            v1 = op(V, lambda e: e.tensor_scalar(tj[:, :], ti[:, :], 127, None, ALU.bitwise_and), v, t2)
            v2 = op(V, lambda e: e.tensor_scalar(adr.bitcast(I32)[:, :], ti[:, :], 7, None, ALU.logical_shift_right), v)
            v = op(V, lambda e: e.scalar_tensor_tensor(out=ti[:, :], in0=tj[:, :], scalar=float(NCH), in1=adr.bitcast(I32)[:, :],
                                                       op0=ALU.mult, op1=ALU.add), v1, v2)
            return op(V, lambda e: e.tensor_copy(adr.bitcast(I32)[:, :], ti[:, :]), v), t3, bk, p2

        def degrees(weighted, use_after):
            w = 2 * NBK if weighted else NBK
            prev, mms = [], []
            for n, c0 in enumerate(range(0, EC, 8)):
                g = min(8, EC - c0)
                B = big[n % 2]
                ol = B[:, 0:8 * P].rearrange("p (g j) -> p g j", g=8)[:, 0:g, :]
                oh = B[:, 8 * P:].rearrange("p (g j) -> p g j", g=8)[:, 0:g, :]
                free = [mms[n - 2]] if n >= 2 else []
                x1 = op(V, lambda e, ol=ol, c0=c0, g=g: e.tensor_tensor(
                    ol, iot[:, :].unsqueeze(1).to_broadcast([P, g, P]),
                    lof[:, c0:c0 + g].unsqueeze(2).to_broadcast([P, g, P]), ALU.is_equal), *free, *use_after)
                x2 = op(V, lambda e, oh=oh, c0=c0, g=g: e.tensor_tensor(
                    oh[:, :, 0:NBK], iot[:, 0:NBK].unsqueeze(1).to_broadcast([P, g, NBK]),
                    hi[:, c0:c0 + g].unsqueeze(2).to_broadcast([P, g, NBK]), ALU.is_equal))
                if weighted:
                    x2 = op(V, lambda e, oh=oh, c0=c0, g=g: e.tensor_tensor(
                        oh[:, :, NBK:2 * NBK], oh[:, :, 0:NBK],
                        we[:, c0:c0 + g].unsqueeze(2).to_broadcast([P, g, NBK]), ALU.mult), x2, *l_we)
                for i in range(g):
                    c = c0 + i
                    m_ = op(T, lambda e, ol=ol, oh=oh, i=i, c=c: e.matmul(
                        PA[2][:, 0:w], ol[:, i, :], oh[:, i, 0:w], start=c == 0, stop=c == EC - 1), x2)
                mms.append(m_)
            return m_

        def scatter(dst, adr, pay, c, s, *waits):
            return dma(G_, lambda e: e.indirect_dma_start(
                dst, bass.IndirectOffsetOnAxis(ap=adr[:, c:c + 1], axis=0), pay, None,
                bounds_check=P * NCH - 1, oob_is_err=False), s, *waits)

        aD, pD, bD, fD = rank(keyi[0], l_dst, keyi[1], l_src, adrD, BKD, payD[:, :, 0], [])
        pW = op(V, lambda e: e.tensor_copy(payD[:, :, 1], we[:, :]), *l_we)
        for c in range(EC):
            sD = scatter(SLOTD, adrD, payD[:, c, :], c, s_sD, aD, pD, pW, z_sd)

        def norm(stats, then, more=[]):
            t = op(V, lambda e: e.tensor_scalar(dk[:, :], mv[:, :, 1], EPS, None, ALU.add), stats[-1], *more)
            t = rsqrt(rstd, dk[:, :], t)
            t = op(V, lambda e: e.scalar_tensor_tensor(out=nmr[:, :], in0=mv[:, :, 0], scalar=-1.0, in1=rstd[:, :],
                                                       op0=ALU.mult, op1=ALU.mult), t)
            for b in range(NBK):
                n_ = op(S, lambda e, b=b: e.activation(X[:, b, :], X[:, b, :], ACT.Identity, bias=nmr[:, b:b + 1],
                                                       scale=rstd[:, b:b + 1]), t)
                then(b, n_)

        def stats_of(b, tok):
            s_ = op(V, lambda e: e.bn_stats(st[:, b, :], X[:, b, :]), tok)
            return op(V, lambda e: e.bn_aggr(mv[:, b, :], st[:, b, :]), s_)

        arv = ACC[:, :, 256:260]
        v = op(V, lambda e: e.tensor_tensor(alb[:, :, :], al[:, :, :], arv, ALU.add), *g0_done)
        v = op(V, lambda e: e.scalar_tensor_tensor(out=al[:, :, :], in0=alb[:, :, :], scalar=0.01, in1=alb[:, :, :],
                                                   op0=ALU.mult, op1=ALU.max), v)
        v = op(V, lambda e: e.tensor_reduce(amx[:, :], al[:, :, :], AX.X, ALU.max), v)
        bc = lambda t_: t_[:, :].unsqueeze(2).to_broadcast([P, NBK, 4])
        v = op(V, lambda e: e.tensor_tensor(alb[:, :, :], al[:, :, :], bc(amx), ALU.subtract), v)
        v = op(S, lambda e: e.activation(al[:, :, :], alb[:, :, :], ACT.Exp), v)
        v = op(V, lambda e: e.tensor_reduce(amx[:, :], al[:, :, :], AX.X, ALU.add), v)
        v = op(V, lambda e: e.reciprocal(dk[:, :], amx[:, :]), v)
        soft = op(V, lambda e: e.tensor_tensor(alb[:, :, :], al[:, :, :], bc(dk), ALU.mult), v)
        stats = []
        for b in range(NBK):
            pr = ACC[:, b, 0:D].rearrange("p (h d) -> p h d", h=4)
            v = op(V, lambda e, pr=pr, b=b: e.tensor_tensor(
                pr, pr, alb[:, b, :].unsqueeze(2).to_broadcast([P, 4, 64]), ALU.mult), soft)
            h_ = hb[b % 3]
            v = op(V, lambda e, b=b, h_=h_: e.tensor_reduce(
                h_[:, 0:64], ACC[:, b, 0:D].rearrange("p (h d) -> p d h", h=4), AX.X, ALU.add), v)
            xv = X[:, b, :].rearrange("p (h d) -> p h d", h=4)
            v = op(V, lambda e, xv=xv, h_=h_: e.tensor_tensor(
                xv, xv, h_[:, 0:64].unsqueeze(1).to_broadcast([P, 4, 64]), ALU.add), v, use["pt"][NBK - 1])
            stats.append(stats_of(b, v))

        mD = degrees(True, [aD, fD])
        v = op(V, lambda e: e.tensor_copy(degI[:, :], PA[2][:, 0:NBK]), mD)
        w_ = op(V, lambda e: e.tensor_scalar(degW[:, :], PA[2][:, NBK:2 * NBK], 1.0, None, ALU.add), mD)
        v2 = op(V, lambda e: e.tensor_scalar(dk[:, :], degI[:, :], 0.0, None, ALU.is_gt), v)
        v3 = op(V, lambda e: e.tensor_scalar(d1[:, :], degI[:, :], 1.0, None, ALU.max), v)
        v3 = rsqrt(d1, d1[:, :], v3)
        k1 = op(V, lambda e: e.tensor_tensor(d1[:, :], d1[:, :], dk[:, :], ALU.mult), v2, v3)
        v2 = op(V, lambda e: e.tensor_scalar(dk[:, :], degW[:, :], 0.0, None, ALU.is_gt), w_, k1)
        v3 = op(V, lambda e: e.tensor_scalar(d2[:, :], degW[:, :], 1e-30, None, ALU.max), w_)
        v3 = rsqrt(d2, d2[:, :], v3)
        k2 = op(V, lambda e: e.tensor_tensor(d2[:, :], d2[:, :], dk[:, :], ALU.mult), v2, v3)

        def unslot(dram, cols, done, bkdram, bk, guard):
            l1 = load(SL[:, :, :].rearrange("p k o -> p (k o)")[:, 0:cols * NCH],
                      dram.rearrange("(p k) o -> p (k o)", p=P), done, *guard)
            l2 = load(row[:, :], bkdram[:, :], bk, *guard)
            pv = SL[:, :, 0] if cols == 2 else SL[:, :, :].rearrange("p k o -> p (k o)")[:, 0:NCH]
            v = op(V, lambda e: e.tensor_copy(idx.bitcast(I32)[:, :], pv), l1, *guard)
            v1 = op(V, lambda e: e.tensor_scalar(dlo.bitcast(I32)[:, :], idx.bitcast(I32)[:, :], 127, None, ALU.bitwise_and), v)
            v2 = op(V, lambda e: e.tensor_copy(dlo[:, :], dlo.bitcast(I32)[:, :]), v1)
            v3 = op(V, lambda e: e.tensor_scalar(idx.bitcast(I32)[:, :], idx.bitcast(I32)[:, :], 7, None,
                                                 ALU.logical_shift_right), v1)
            return [v2, v3, l2]

        regs = {}
        hist = {"gfree": [], "mfree": [], "afree": []}

        def aggregate(table, weighted, ready):
            gs, ms, mm_, adds = [], [], [], []

            def add(k):
                if k % 4 == 0:
                    def ld(e, k=k):
                        rs = regs.setdefault((k // 4) % 2, [e.alloc_register(f"bk{(k // 4) % 2}_{i}") for i in range(4)]
                                             if (k // 4) % 2 not in regs else None)
                        e.load(rs, row[0:1, k:k + 4])
                        regs["v"] = [e.snap(r_, min_val=0, max_val=AW * (NBK - 1)) for r_ in rs]
                    q.plain(V, ld, *ready)
                accf = ACC[:, :, :].rearrange("p b w -> p (b w)")

                def fn(e, k=k):
                    o = accf[:, bass.ds(regs["v"][k % 4], D)]
                    return e.tensor_tensor(o, o, PA[k % NA][:, 0:D], ALU.add)
                adds.append(op(V, fn, mm_[k], *adds[-1:]))
            for k in range(NCH):
                gf = [mm_[k - NG]] if k >= NG else hist["gfree"]
                gs.append(dma(G_, lambda e, k=k: e.indirect_dma_start(
                    G[k % NG][:, :], None, table, bass.IndirectOffsetOnAxis(ap=idx[:, k:k + 1], axis=0)),
                    s_g[k % NG], *gf, *ready))
                mf = [mm_[k - NM]] if k >= NM else hist["mfree"]
                if weighted:
                    fn = lambda e, k=k: e.tensor_scalar(M[k % NM][:, :], iot[:, :], dlo[:, k:k + 1], SL[:, k, 1:2],
                                                        ALU.is_equal, ALU.mult)
                else:
                    fn = lambda e, k=k: e.tensor_scalar(M[k % NM][:, :], iot[:, :], dlo[:, k:k + 1], None, ALU.is_equal)
                ms.append(op(V, fn, *mf, *ready))
                af = [adds[k - NA]] if k >= NA else hist["afree"]
                mm_.append(op(T, lambda e, k=k: e.matmul(PA[k % NA][:, 0:D], M[k % NM][:, :], G[k % NG][:, :],
                                                        start=True, stop=True), gs[k], ms[k], *af))
                if k >= 2:
                    add(k - 2)
            add(NCH - 2)
            add(NCH - 1)
            hist["gfree"], hist["mfree"], hist["afree"] = [mm_[-1]], [mm_[-1]], [adds[-1]]
            return adds[-1]

        def table_from(scale, TAB, Wt, wtok):
            toks = []

            def make(b, tok, src=None):
                src = X[:, b, :] if src is None else src

                def evac(ph, mt):
                    t = op(V, lambda e: e.tensor_scalar(ACC[:, b, 0:D], ph[:, 0:D], scale[:, b:b + 1], None, ALU.mult), mt)
                    r = rows_of(b)
                    toks.append(dma("sync", lambda e: e.dma_start(TAB[1 + b * P:1 + b * P + r, :], ACC[0:r, b, 0:D]),
                                    s_st[b % 2], t))
                    return t
                return project(src, Wt, D, [tok, *wtok], evac)
            return toks, make

        s_cursor = [0]

        def scatter_src(n, *waits):
            t = None
            for c in range(s_cursor[0], min(EC, s_cursor[0] + n)):
                t = scatter(SLOTS, adrD, payD[:, c, 0:1], c, s_sS, *waits)
            s_cursor[0] += n
            return t

        toks, then = table_from(d1, T1, W1, l_w)
        norm(stats, then, [k1, k2])
        rdD = unslot(SLOTD, 2, sD, BKD, bD, [z_sd, z_ss, *z_rows])
        last = toks[-1]
        zacc = op(V, lambda e: e.memset(ACC[:, :, 0:D], 0.0), *toks[-2:])
        done = aggregate(T1, False, [*toks[-2:], *z_rows, *rdD, zacc])

        aS, pS, bS, fS = rank(keyi[1], l_src, keyi[0], l_dst, adrD, BKS, payD[:, :, 0], [mD, sD, done])
        mS = degrees(False, [aS, fS])
        v = op(V, lambda e: e.tensor_copy(degS[:, :], PA[2][:, 0:NBK]), mS)
        v = op(V, lambda e: e.tensor_scalar(degS[:, :], degS[:, :], 1.0, None, ALU.add), v)
        k3 = rsqrt(d3, degS[:, :], v)
        hist["afree"] = [v, k3]

        def residual(scale, done_):
            out_ = []
            for b in range(NBK):
                v = op(V, lambda e, b=b: e.scalar_tensor_tensor(out=X[:, b, :], in0=ACC[:, b, 0:D], scalar=scale[:, b:b + 1],
                                                                in1=X[:, b, :], op0=ALU.mult, op1=ALU.add), done_)
                out_.append(stats_of(b, v))
            return out_

        stats = residual(d1, done)
        toks, then = table_from(d2, T2, W2, l_w)
        norm(stats, then, [k2])
        scatter_src(EC // 3, aS, pS, z_ss)
        done = aggregate(T2, True, [*toks[-2:], *z_rows])

        toks, then = table_from(d2, T3, W3, l_w)
        tr = []
        for b in range(NBK):
            h_ = hb[b % 3]
            v = op(V, lambda e, b=b, h_=h_: e.scalar_tensor_tensor(out=h_[:, :], in0=ACC[:, b, 0:D], scalar=d2[:, b:b + 1],
                                                                   in1=b1[:, :], op0=ALU.mult, op1=ALU.add),
                   done, *l_b, *([tr[b - 3]] if b >= 3 else []))
            v = op(S, lambda e, h_=h_: e.activation(h_[:, :], h_[:, :], ACT.Relu), v)
            tr.append(then(b, v, h_[:, :]))
        scatter_src(EC // 3, aS, pS, z_ss)
        done = aggregate(T3, True, [*toks[-2:], *z_rows])
        stats = []
        for b in range(NBK):
            h_ = hb[b % 3]
            v = op(V, lambda e, b=b, h_=h_: e.scalar_tensor_tensor(out=h_[:, :], in0=ACC[:, b, 0:D], scalar=d2[:, b:b + 1],
                                                                   in1=b2[:, :], op0=ALU.mult, op1=ALU.add), done, tr[-1])
            v = op(V, lambda e, b=b, h_=h_: e.scalar_tensor_tensor(out=X[:, b, :], in0=h_[:, :], scalar=0.0, in1=X[:, b, :],
                                                                   op0=ALU.max, op1=ALU.add), v)
            stats.append(stats_of(b, v))
        for i in range(2):
            for j in range(2):
                n = 2 * i + j
                t = op(T, lambda e, i=i, j=j: e.transpose(PA[i][:, j * P:(j + 1) * P], W4r[:, j, i * P:(i + 1) * P],
                                                          ident[:, :]), *l_w, *hist["afree"])
            wt = op(S, lambda e, i=i: e.copy(W4[:, i, 0:D], PA[i][:, 0:D]), t)
        hist["afree"] = hist["afree"] + [wt]
        toks, then = table_from(d3, T4, W4, [wt])
        norm(stats, then, [k3])
        sS = scatter_src(EC, aS, pS, z_ss)
        rdS = unslot(SLOTS, 1, sS, BKS, bS, [done])
        done = aggregate(T4, False, [*toks[-2:], *z_rows, *rdS])
        stats = residual(d3, done)

        def store(b, tok):
            r = rows_of(b)
            dma("sync", lambda e: e.dma_start(out[b * P:b * P + r, :], X[0:r, b, :]), s_out, tok)
        norm(stats, store)
        q.plain("sync", lambda e: e.wait_ge(s_out, q.dma_n[s_out]))

        block = ctx.enter_context(nc.Block())
        block.sync(lambda e: q.run("sync", e))
        block.vector(lambda e: q.run("vector", e))
        block.scalar(lambda e: q.run("scalar", e))
        block.tensor(lambda e: q.run("tensor", e))
        block.gpsimd(lambda e: q.run("gpsimd", e))


def kernel(**inputs):
    import numpy as np
    import concourse.bacc as bacc
    from concourse.bass_utils import run_bass_kernel_spmd as run
    nc = bacc.Bacc("TRN2", target_bir_lowering=False, num_devices=1)
    arrays, args = {}, {}
    for name, v in inputs.items():
        v = np.ascontiguousarray(v)
        arrays[f"in_{name}"] = v
        args[name] = nc.dram_tensor(f"in_{name}", v.shape, mybir.dt.from_np(v.dtype), kind="ExternalInput").ap()
    out = nc.dram_tensor("out_0", (N, D), F32, kind="ExternalOutput").ap()
    program(nc, args, out)
    r = run(nc, [arrays], core_ids=[0])
    return r.results[0]["out_0"]
```

```python
from contextlib import ExitStack

import concourse.bass as bass
from concourse import mybir

F32 = mybir.dt.float32
BF16 = mybir.dt.bfloat16
I32 = mybir.dt.int32
U32 = mybir.dt.uint32
U16 = mybir.dt.uint16
ALU = mybir.AluOpType
ACT = mybir.ActivationFunctionType
AX = mybir.AxisListType

N, D, E = 6250, 256, 106250
P = 128
NBK = 49
LAST = N - (NBK - 1) * P
EC = 831
ETAIL = E - (P - 1) * EC
NCH = E // P + NBK + 1
KC = 896
PADN = (KC - E // P + 1) * P
AW = 264
EPS = 1e-5
NG, NM, NA = 7, 4, 4
UNSLOTTED = float(127 + 128 * 1000)
F16 = mybir.dt.float16
T0_FIRST = 20


class Queues:

    def __init__(self, sems):
        self.sem = sems
        self.n = {e: 0 for e in sems}
        self.dma_n = {}
        self.seen = {e: {} for e in list(sems) + ["sync"]}
        self.code = {e: [] for e in list(sems) + ["sync"]}

    def _waits(self, eng, waits):
        out = []
        for sem, val in waits:
            if self.seen[eng].get(sem, 0) < val:
                self.seen[eng][sem] = val
                out.append((sem, val))
        return out

    def op(self, eng, fn, *waits):
        self.n[eng] += 1
        self.code[eng].append((self._waits(eng, waits), fn, self.sem[eng], 1))
        return (self.sem[eng], self.n[eng])

    def dma(self, eng, fn, sem, *waits):
        self.dma_n[sem] = self.dma_n.get(sem, 0) + 16
        self.code[eng].append((self._waits(eng, waits), fn, sem, 16))
        return (sem, self.dma_n[sem])

    def plain(self, eng, fn, *waits):
        self.code[eng].append((self._waits(eng, waits), fn, None, 0))

    def branch(self, engines, inner, flag, *waits):
        for name in engines:
            def fn(eng, name=name):
                with eng.If(eng.value_load(flag, min_val=0, max_val=1) < 1):
                    inner.run(name, eng)
            self.plain(name, fn, *waits)

    def run(self, name, eng):
        for waits, fn, sem, by in self.code[name]:
            for s, v in waits:
                eng.wait_ge(s, v)
            ins = fn(eng)
            if sem is not None:
                ins.then_inc(sem, by)


def program(nc, a, out):
    dr = lambda n, s, d=F32: nc.dram_tensor(n, s, d, kind="Internal").ap()
    T0, T1, T2, T3, T4 = (dr("T0", (N, 260)), dr("T1", (N + 1, D)), dr("T2", (N + 1, D)),
                          dr("T3", (N + 1, D)), dr("T4", (N + 1, D)))
    TL = dr("TL", (N, 4))
    SLOTD = dr("SLOTD", (P * NCH, 2))
    LD, LS, LW = dr("LD", (E + PADN, 1), I32), dr("LS", (E + PADN, 1), I32), dr("LW", (E + PADN, 1))
    BKD, BKS = dr("BKD", (1, KC), I32), dr("BKS", (1, KC), I32)
    with ExitStack() as ctx:
        sb = lambda n, s, d=F32: ctx.enter_context(nc.sbuf_tensor(n, s, d))
        sem = lambda n: ctx.enter_context(nc.semaphore(n))
        X = sb("X", [P, NBK, D])
        ACC = sb("ACC", [P, NBK, AW])
        iot = sb("iot", [P, P])
        pid = sb("pid", [P, 1])
        ident = sb("ident", [P, P])
        lower = sb("lower", [P, P])
        ones = sb("ones", [P, P])
        kio = sb("kio", [P, 7])
        irep = sb("irep", [P, P, 8], F16)
        iok = sb("iok", [P, KC], F16)
        W0 = sb("W0", [P, 2, AW])
        W1, W2, W3, W4r = (sb(f"Wt{i}", [P, 2, D]) for i in range(4))
        W4 = W0
        b1, b2 = (sb(f"bc{i}", [P, D]) for i in range(2))
        hb = [sb(f"hb{i}", [P, D]) for i in range(3)]
        atl, atr, wtmp = hb
        keyi = [sb(f"keyi{i}", [P, EC], I32) for i in range(2)]
        we = sb("we", [P, EC])
        hi = sb("hi", [P, EC], F16)
        lof = sb("lof", [P, EC], F16)
        zb = sb("zb", [P, EC], BF16)
        mm = [sb(f"mm{i}", [P, EC], BF16) for i in range(2)]
        sc = [sb(f"sc{i}", [P, KC]) for i in range(2)]
        ti, tj = (t_[:, 0:EC].bitcast(I32) for t_ in sc)
        rk = sb("rk", [P, KC])
        cnt = sb("cnt", [P, NBK])
        s49 = [sb(f"s49{i}", [P, NBK]) for i in range(5)]
        i49 = [sb(f"i49{i}", [P, NBK], I32) for i in range(2)]
        bks7, bkst = sb("bks7", [P, 7]), sb("bkst", [P, 7])
        bki = sb("bki", [P, 7], I32)
        sti = sb("sti", [P, 7], I32)
        scr = sb("scr", [P, 4 * 832])
        big = [sb(f"big{i}", [P, 8 * (P + NBK)], F16) for i in range(2)]
        wD = sb("wD", [P, KC])
        idx = sb("idx", [P, KC], U32)
        dlo = sb("dlo", [P, KC])
        row = sb("row", [1, KC], I32)
        flag = sb("flag", [1, 1], I32)
        srcN = sb("srcN", [P, NBK], I32)
        dstN = sb("dstN", [P, NBK], I32)
        degI, degS = sb("degI", [P, NBK]), sb("degS", [P, NBK])
        d1, d2, d3, dk = (sb(f"d{i}", [P, NBK]) for i in range(4))
        G = [sb(f"G{i}", [P, D + 1]) for i in range(NG)]
        M = [sb(f"M{i}", [P, P]) for i in range(NM)]
        xT = [sb(f"xT{i}", [P, 2, P]) for i in range(3)]
        M2 = [sb(f"M2{i}", [P, P]) for i in range(2)]
        st = sb("st", [P, NBK, 6])
        mv = sb("mv", [P, NBK, 2])
        rstd, nmr = sb("rstd", [P, NBK]), sb("nmr", [P, NBK])
        rq = [sb(f"rq{i}", [P, NBK]) for i in range(4)]
        al = sb("al", [P, NBK, 4])
        alb = sb("alb", [P, NBK, 4])
        amx = sb("amx", [P, NBK])
        tot = sb("tot", [P, 1])
        PA = [ctx.enter_context(nc.psum_tensor(f"PA{i}", [P, 512], F32)) for i in range(NA)]
        PT = [ctx.enter_context(nc.psum_tensor(f"PT{i}", [P, 512], F32)) for i in range(2)]
        PH = [ctx.enter_context(nc.psum_tensor(f"PH{i}", [P, 512], F32)) for i in range(2)]
        q = Queues({e: sem(f"s_{e}") for e in ("vector", "scalar", "tensor", "gpsimd")})
        fb = Queues({e: sem(f"f_{e}") for e in ("vector", "scalar", "tensor", "gpsimd")})
        op, dma = q.op, q.dma
        V, S, T, G_ = "vector", "scalar", "tensor", "gpsimd"
        s_g = [sem(f"s_g{i}") for i in range(NG)]
        s_st = [sem(f"s_st{i}") for i in range(2)]
        s_sD, s_out, s_sl = sem("s_sD"), sem("s_out"), sem("s_sl")
        s_l0 = [sem(f"s_l0{i}") for i in range(7)]
        ndma = [0]

        def load(dst, src, *waits, eng="sync", slow=False, queue=None):
            ndma[0] += 1
            return (queue or q).dma(eng, lambda e: e.dma_start(dst, src, allow_slow_non_contiguous=slow),
                                    sem(f"s_ld{ndma[0]}"), *waits)

        def rsqrt(dst, src, sl, tok, op=op):
            r = [t_[:, sl] for t_ in rq]
            t = op(S, lambda e: e.activation(r[0], src, ACT.Sqrt), tok)

            def rest():
                t1 = op(V, lambda e: e.reciprocal(r[1], r[0]), t)
                u = op(V, lambda e: e.tensor_tensor(r[2], r[1], r[1], ALU.mult), t1)
                u = op(V, lambda e: e.scalar_tensor_tensor(out=r[3], in0=src, scalar=-0.5, in1=r[2],
                                                           op0=ALU.mult, op1=ALU.mult), u)
                return op(V, lambda e: e.scalar_tensor_tensor(out=dst[:, sl], in0=r[3], scalar=1.5, in1=r[1],
                                                              op0=ALU.add, op1=ALU.mult), u)
            return rest
        ALL = slice(0, NBK)

        io = lambda t_, pat, cm: op(G_, lambda e: e.iota(t_, pat, base=0, channel_multiplier=cm,
                                                         allow_small_or_imprecise_dtypes=True))
        c_iot = io(iot[:, :], [[1, P]], 0)
        c_pid = io(pid[:, :], [[1, 1]], 1)
        c_kio = io(kio[:, :], [[1, 7]], 7)
        c_rep = io(irep[:, :, :], [[1, P], [0, 8]], 0)
        c_iok = io(iok[:, :], [[1, KC]], 0)
        z_key = [op(V, lambda e, i=i: e.memset(keyi[i][96:128, ETAIL:EC], 8192)) for i in range(2)]
        z_idx = op(V, lambda e: e.memset(srcN[:, NBK - 1:NBK], 0))
        z_idx = op(V, lambda e: e.memset(dstN[:, NBK - 1:NBK], 0))
        z_we = op(V, lambda e: e.memset(we[96:128, ETAIL:EC], 0.0))
        z_x = op(V, lambda e: e.memset(X[96:128, NBK - 1, :], 0.0))
        z_p1 = op(V, lambda e: e.memset(sc[0][:, 0:PADN // P].bitcast(I32), 8192))
        z_p0 = op(V, lambda e: e.memset(sc[1][:, 0:256], 0.0))
        c_zb = op(V, lambda e: e.memset(zb[:, :], 0.0))
        c_on = op(V, lambda e: e.memset(ones[:, :], 1.0))

        def load_edges(dst, src, z):
            return [load(dst[0:112, :], src[0:112 * EC].rearrange("(p c) -> p c", c=EC), z),
                    load(dst[112:127, :], src[112 * EC:127 * EC].rearrange("(p c) -> p c", c=EC), z),
                    load(dst[127:128, 0:ETAIL], src[127 * EC:E].rearrange("(p c) -> p c", p=1), z)]

        l_w0 = load(W0[:, :, 0:D], a["L0_gnn_weight"].rearrange("(t p) d -> p t d", p=P), eng=S)
        l_dst = load_edges(keyi[0], a["dst"], z_key[0])
        l_at = [load(t_[:, :], a[n_].rearrange("(o h) d -> o (h d)", o=1).to_broadcast([P, D]), eng=S)
                for t_, n_ in ((atl, "L0_gnn_attn_l"), (atr, "L0_gnn_attn_r"))]
        l_x = [load(X[:, 6 * i:6 * i + 6, :], a["x"][6 * i * P:(6 * i + 6) * P, :].rearrange("(b p) d -> p b d", p=P))
               for i in range(8)] + [load(X[0:LAST, 48, :], a["x"][48 * P:N, :], z_x)]
        l_pad = []
        for t_, n_, pad, z in ((LD, "dst", sc[0][:, 0:PADN // P].bitcast(I32), z_p1),
                               (LS, "src", sc[1][:, 0:PADN // P].bitcast(I32), z_p0),
                               (LW, "edge_weight", sc[1][:, 0:PADN // P], z_p0)):
            l_pad.append(load(t_[0:E, :].rearrange("(p c) o -> p (c o)", p=125),
                              a[n_].rearrange("(p c) -> p c", p=125), eng=S))
            l_pad.append(load(t_[E:E + PADN, :].rearrange("(p c) o -> p (c o)", p=P), pad, z, eng=S))
        l_nodes = []
        for t_, n_ in ((srcN, "src"), (dstN, "dst")):
            l_nodes.append(load(t_[:, 0:48], a[n_][0:48 * P].rearrange("(b p) -> p b", p=P), slow=True))
            l_nodes.append(load(t_[0:LAST, 48:49], a[n_][48 * P:N].rearrange("(p o) -> p o", o=1), z_idx, slow=True))
        l_src = load_edges(keyi[1], a["src"], z_key[1])
        l_we = load_edges(we, a["edge_weight"], z_we)
        l_w = [load(t_[:, :, :], a[n_].rearrange("(t p) d -> p t d", p=P), eng=S)
               for t_, n_ in ((W1, "L1_gnn_W"), (W2, "L2_gnn_W1"), (W3, "L2_gnn_W2"), (W4r, "L3_gnn_W"))]
        l_b = [load(t_[:, :], a[n_].rearrange("(o d) -> o d", o=1).to_broadcast([P, D]), eng=S)
               for t_, n_ in ((b1, "L2_gnn_b1"), (b2, "L2_gnn_b2"))]
        z_rows = [load(t_[0:1, :], sc[1][0:1, 0:D], z_p0, eng=S) for t_ in (T1, T2, T3, T4)]

        c_id = op(V, lambda e: e.tensor_scalar(ident[:, :], iot[:, :], pid[:, 0:1], None, ALU.is_equal), c_pid, c_iot)
        c_lo = op(V, lambda e: e.tensor_scalar(lower[:, :], iot[:, :], pid[:, 0:1], None, ALU.is_gt))

        wa = []
        for t in range(2):
            for col, at in ((256, atr), (260, atl)):
                m_ = op(V, lambda e, t=t, at=at: e.tensor_tensor(wtmp[:, :], W0[:, t, 0:D], at[:, :], ALU.mult),
                        l_w0, *l_at, *wa)
                wa = [op(V, lambda e, t=t, col=col: e.tensor_reduce(
                    W0[:, t, col:col + 4], wtmp[:, :].rearrange("p (h d) -> p h d", h=4), AX.X, ALU.add), m_)]

        use = {"pt": [], "ph": [], "xt": []}
        held = []

        def multiply():
            xt, ph, Wt, width, cp, evac = held.pop(0)
            n = len(use["ph"])
            w_ph = [use["ph"][n - 2]] if n >= 2 else []
            for t in range(2):
                mt = op(T, lambda e, t=t: e.matmul(ph[:, 0:width], xt[:, t, :], Wt[:, t, 0:width],
                                                  start=t == 0, stop=t == 1), cp, *w_ph)
            use["xt"].append(mt)
            use["ph"].append(evac(ph, mt))

        def project(src_ap, Wt, width, ready, evac):
            n = len(use["pt"])
            pt, ph, xt = PT[n % 2], PH[n % 2], xT[n % 3]
            w_pt = [use["pt"][n - 2]] if n >= 2 else []
            op(T, lambda e: e.transpose(pt[:, 0:P], src_ap[:, 0:P], ident[:, :]), c_id, *ready, *w_pt)
            tr = op(T, lambda e: e.transpose(pt[:, P:2 * P], src_ap[:, P:2 * P], ident[:, :]))
            w_xt = [use["xt"][n - 3]] if n >= 3 else []
            cp = op(S, lambda e: e.copy(xt[:, :, :].rearrange("p t n -> p (t n)"), pt[:, 0:2 * P]), tr, *w_xt)
            use["pt"].append(cp)
            if held:
                multiply()
            held.append((xt, ph, Wt, width, cp, evac))
            return tr

        def rows_of(b):
            return LAST if b == NBK - 1 else P

        def split(key, lk, guard, op=op):
            t = op(V, lambda e: e.tensor_scalar(ti[:, :], key[:, :], 7, None, ALU.logical_shift_right), *lk, *guard)
            t1 = op(V, lambda e: e.tensor_copy(hi[:, :], ti[:, :]), t)
            t2 = op(V, lambda e: e.tensor_scalar(tj[:, :], key[:, :], 127, None, ALU.bitwise_and))
            return [t1, op(V, lambda e: e.tensor_copy(lof[:, :], tj[:, :]), t2)]

        def chunk_map(res, banks, key_tok, guard, op=op, starts=False):
            b0, b1_ = banks
            counts = []
            for b in range(NBK):
                w_ = [counts[b - 2]] if b >= 2 else []
                counts.append(op(V, lambda e, b=b: e.tensor_scalar(
                    mm[b % 2][:, :], hi[:, :], float(b), 0.0, ALU.is_equal, ALU.add, accum_out=cnt[:, b:b + 1]),
                    *key_tok, *w_, *guard))
                yield 0.5
            p1 = op(T, lambda e: e.matmul(b0[:, 0:NBK], lower[:, :], cnt[:, :], start=True, stop=True), counts[-1], c_lo, *guard)
            p2 = op(T, lambda e: e.matmul(b1_[:, 0:NBK], ones[:, :], cnt[:, :], start=True, stop=True), c_on)
            v = op(V, lambda e: e.tensor_scalar(i49[0][:, :], b1_[:, 0:NBK], 127.0, None, ALU.add), p2)
            v = op(V, lambda e: e.tensor_scalar(i49[1][:, :], i49[0][:, :], 7, None, ALU.logical_shift_right), v)
            v = op(V, lambda e: e.tensor_copy(s49[0][:, :], i49[1][:, :]), v)
            incl = op(V, lambda e: e.tensor_tensor_scan(s49[1][:, :], s49[0][:, :], zb[:, 0:NBK], 0.0, ALU.add, ALU.add), v, c_zb)
            v = op(V, lambda e: e.tensor_tensor(s49[2][:, :], s49[1][:, :], s49[0][:, :], ALU.subtract), incl)
            v = op(V, lambda e: e.tensor_scalar(s49[3][:, :], s49[2][:, :], 128.0, -1.0, ALU.mult, ALU.add), v)
            res["base"] = op(V, lambda e: e.tensor_tensor(s49[4][:, :], b0[:, 0:NBK], s49[3][:, :], ALU.add), v, p1)
            yield 2.0
            le = rk[:, 0:7 * NBK].rearrange("p (t b) -> p t b", t=7)
            u = op(V, lambda e: e.tensor_tensor(
                le, s49[1][:, :].unsqueeze(1).to_broadcast([P, 7, NBK]),
                kio[:, :].unsqueeze(2).to_broadcast([P, 7, NBK]), ALU.is_le), incl, c_kio)
            bt = op(V, lambda e: e.tensor_reduce(bks7[:, :], le, AX.X, ALU.add), u)
            u = op(V, lambda e: e.tensor_scalar(bki[:, :], bks7[:, :], float(NBK - 1), float(AW), ALU.min, ALU.mult), bt)
            res["bki"] = u
            if starts:
                v = op(V, lambda e: e.scalar_tensor_tensor(out=s49[2][:, :], in0=s49[0][:, :], scalar=-128.0,
                                                           in1=b1_[:, 0:NBK], op0=ALU.mult, op1=ALU.add), v)
                v = op(V, lambda e: e.tensor_tensor(le, le, s49[2][:, :].unsqueeze(1).to_broadcast([P, 7, NBK]), ALU.mult),
                       v, bt)
                v = op(V, lambda e: e.tensor_reduce(bkst[:, :], le, AX.X, ALU.add), v)
                v = op(V, lambda e: e.scalar_tensor_tensor(out=sti[:, :], in0=kio[:, :], scalar=128.0, in1=bkst[:, :],
                                                           op0=ALU.mult, op1=ALU.add), v)
                res["starts"] = v
            res["free"] = [u, v, p2]
            yield 1.5

        def slots(res, op=op, after=[]):
            r0 = op(V, lambda e: e.memset(rk[:, :], UNSLOTTED), *res["free"], *after)
            prev = []
            for b in range(NBK):
                m_ = op(V, lambda e, b=b: e.tensor_scalar(mm[b % 2][:, :], hi[:, :], float(b), None, ALU.is_equal),
                        *(res["free"] if b == 0 else []), *prev[-2:-1], *after)
                s_ = op(V, lambda e, b=b: e.tensor_tensor_scan(sc[b % 2][:, 0:EC], mm[b % 2][:, :], zb[:, :],
                                                              s49[4][:, b:b + 1], ALU.add, ALU.add), m_, res["base"], *after)
                prev.append(op(V, lambda e, b=b: e.copy_predicated(rk[:, 0:EC], mm[b % 2][:, :].bitcast(U16),
                                                                  sc[b % 2][:, 0:EC]), s_, r0, *prev[-1:]))
                yield 3.0
            res["slots"] = prev[-1]

        def degrees(res, bank, after, lag=1):
            groups, mms = [], []

            def products(n):
                x2, ol, oh, c0, g = groups[n]
                for i in range(g):
                    c = c0 + i
                    m_ = op(T, lambda e, ol=ol, oh=oh, i=i, c=c: e.matmul(
                        bank[:, 0:NBK], ol[:, :, i], oh[:, :, i], start=c == 0, stop=c == EC - 1), x2, *after)
                mms.append(m_)
            for n, c0 in enumerate(range(0, EC, 8)):
                g = min(8, EC - c0)
                B = big[n % 2]
                ol = B[:, 0:g * P].rearrange("p (j g) -> p j g", g=g)
                oh = B[:, 8 * P:8 * P + g * NBK].rearrange("p (j g) -> p j g", g=g)
                free = [mms[n - 2]] if n >= 2 else []
                op(V, lambda e, ol=ol, c0=c0, g=g: e.tensor_tensor(
                    ol, irep[:, :, 0:g], lof[:, c0:c0 + g].unsqueeze(1).to_broadcast([P, P, g]), ALU.is_equal),
                    *free, *after, c_rep)
                x2 = op(V, lambda e, oh=oh, c0=c0, g=g: e.tensor_tensor(
                    oh, irep[:, 0:NBK, 0:g], hi[:, c0:c0 + g].unsqueeze(1).to_broadcast([P, NBK, g]), ALU.is_equal))
                groups.append((x2, ol, oh, c0, g))
                if n >= lag:
                    products(n - lag)
                yield 0.95
            for n in range(len(groups) - lag, len(groups)):
                products(n)
            res["deg"] = mms[-1]

        def finish(gen):
            for _ in gen:
                pass

        t0_st = {}

        def t0_block(b):
            r = rows_of(b)

            def evac(ph, mt):
                t = op(S, lambda e: e.copy(ACC[:, b, 0:264], ph[:, 0:264]), mt)
                t0_st[0] = dma("sync", lambda e: e.dma_start(T0[b * P:b * P + r, :], ACC[0:r, b, 0:260]), s_st[0], t)
                t0_st[1] = dma("sync", lambda e: e.dma_start(TL[b * P:b * P + r, :], ACC[0:r, b, 260:264]), s_st[1], t)
                return t
            project(X[:, b, :], W0, 264, [l_x[b // 6], *wa], evac)

        for b in range(T0_FIRST):
            t0_block(b)
        hk = split(keyi[0], l_dst, [*l_pad, *z_rows])
        rD = {}
        finish(chunk_map(rD, (PA[0], PA[1]), hk, [], starts=True))
        KD, KS = (scr[:, i * KC:(i + 1) * KC].bitcast(I32) for i in range(2))
        KW = scr[:, 2 * KC:3 * KC]
        sl = []
        for t_, dram, i32 in ((KD, LD, 1), (KS, LS, 1), (KW, LW, 0)):
            for t in range(7):
                s_ = dma(G_, lambda e, t_=t_, dram=dram, t=t: e.indirect_dma_start(
                    t_[:, t * P:(t + 1) * P], None, dram,
                    bass.IndirectOffsetOnAxis(ap=sti[:, t:t + 1].bitcast(U32), axis=0)), s_sl, rD["starts"], *l_pad)
        for b in range(T0_FIRST, NBK):
            t0_block(b)
        multiply()
        t0_done = [t0_st[0], t0_st[1]]
        g0 = []
        for b in range(NBK):
            dma(G_, lambda e, b=b: e.indirect_dma_start(
                ACC[:, b, 0:260], None, T0, bass.IndirectOffsetOnAxis(ap=dstN[:, b:b + 1].bitcast(U32), axis=0)),
                s_l0[b // 7], *t0_done, *l_nodes)
            g0.append(dma(G_, lambda e, b=b: e.indirect_dma_start(
                al[:, b, :], None, TL, bass.IndirectOffsetOnAxis(ap=srcN[:, b:b + 1].bitcast(U32), axis=0)),
                s_l0[b // 7], *t0_done, *l_nodes))

        finish(degrees(rD, PA[3], hk))
        v = op(V, lambda e: e.tensor_copy(degI[:, :], PA[3][:, 0:NBK]), rD["deg"])
        v2 = op(V, lambda e: e.tensor_scalar(dk[:, :], degI[:, :], 0.0, None, ALU.is_gt), v)
        v = op(V, lambda e: e.tensor_scalar(degI[:, :], degI[:, :], 1.0, None, ALU.max), v2)
        v = rsqrt(d1, degI[:, :], ALL, v)()
        k1 = op(V, lambda e: e.tensor_tensor(d1[:, :], d1[:, :], dk[:, :], ALU.mult), v2, v)

        bt7 = bks7[:, :].unsqueeze(2).to_broadcast([P, 7, P])
        v3 = lambda t_: t_.rearrange("p (t n) -> p t n", t=7)
        scf = [t_[:, :] for t_ in sc]
        v = op(V, lambda e: e.tensor_scalar(scf[0].bitcast(I32), KD, 7, None, ALU.logical_shift_right), s_, *hk, *l_pad)
        v = op(V, lambda e: e.tensor_copy(scf[1], scf[0].bitcast(I32)), v, *z_rows)
        msk = op(V, lambda e: e.tensor_tensor(v3(rk[:, :]), v3(scf[1]), bt7, ALU.is_equal), v, *rD["free"])
        val = op(V, lambda e: e.scalar_tensor_tensor(out=scf[0], in0=KS, scalar=1.0, in1=rk[:, :],
                                                     op0=ALU.add, op1=ALU.mult), msk)
        wv = op(V, lambda e: e.tensor_tensor(KW, KW, rk[:, :], ALU.mult), msk)
        tt = op(V, lambda e: e.tensor_reduce(tot[:, :], rk[:, :], AX.X, ALU.add), msk)
        v = op(V, lambda e: e.tensor_scalar(KD, KD, 127, None, ALU.bitwise_and))
        lv = op(V, lambda e: e.tensor_copy(scf[1], KD), v, msk)
        pt_ = op(T, lambda e: e.matmul(PA[0][:, 0:1], ones[:, :], tot[:, :], start=True, stop=True), tt, rD["base"])
        fl = op(V, lambda e: e.tensor_scalar(flag[:, :], PA[0][0:1, 0:1], float(E), None, ALU.is_equal), pt_)
        l_row = []
        bkl = load(BKD.rearrange("o (p t) -> (o p) t", t=7), bki[:, :], rD["bki"])
        cps = []
        for i, (src_, dst_, tk) in enumerate(((scf[0], idx[:, :], val), (scf[1], dlo[:, :], lv), (KW, wD[:, :], wv))):
            for h, (ta, tb) in enumerate(((0, 4), (4, 7))):
                bank = PA[(2 * i + h) % 3 + 1]
                g_ = [cps[2 * i + h - 3]] if 2 * i + h >= 3 else [rD["free"][1], k1]
                for t in range(ta, tb):
                    tr = op(T, lambda e, t=t, ta=ta, bank=bank, src_=src_: e.transpose(
                        bank[:, (t - ta) * P:(t - ta + 1) * P], src_[:, t * P:(t + 1) * P], ident[:, :]), tk, *g_)
                dv = dst_.rearrange("p (k t) -> p t k", t=7)[:, ta:tb, :]
                cps.append(op(V, lambda e, dv=dv, bank=bank, ta=ta, tb=tb: e.tensor_copy(
                    dv, bank[:, 0:(tb - ta) * P].rearrange("p (t k) -> p t k", k=P)), tr))
        def stats_of(b, tok):
            s_ = op(V, lambda e: e.bn_stats(st[:, b, :], X[:, b, :]), tok)
            return op(V, lambda e: e.bn_aggr(mv[:, b, :], st[:, b, :]), s_)

        def transition(residual, then, more=[]):
            tok = {}
            for g in range(8):
                for i in range(7):
                    if g < 7:
                        stt = stats_of(7 * g + i, residual(g, 7 * g + i))
                    if g < 7 and i == 6:
                        s7 = slice(7 * g, 7 * g + 7)
                        t = op(V, lambda e, s7=s7: e.tensor_scalar(dk[:, s7], mv[:, s7, 1], EPS, None, ALU.add), stt, *more)
                        rest = rsqrt(rstd, dk[:, s7], s7, t)
                    if g > 0:
                        then(7 * (g - 1) + i, tok[7 * (g - 1) + i])
                if g < 7:
                    t = rest()
                    t = op(V, lambda e, s7=s7: e.scalar_tensor_tensor(out=nmr[:, s7], in0=mv[:, s7, 0], scalar=-1.0,
                                                                      in1=rstd[:, s7], op0=ALU.mult, op1=ALU.mult), t)
                    for b in range(7 * g, 7 * g + 7):
                        tok[b] = op(S, lambda e, b=b: e.activation(X[:, b, :], X[:, b, :], ACT.Identity,
                                                                   bias=nmr[:, b:b + 1], scale=rstd[:, b:b + 1]), t)

        soft = {}

        def softmax(g):
            s7 = slice(7 * g, 7 * g + 7)
            A_, B_ = al[:, s7, :], alb[:, s7, :]
            bc = lambda t_: t_[:, s7].unsqueeze(2).to_broadcast([P, 7, 4])
            v = op(V, lambda e: e.tensor_tensor(B_, A_, ACC[:, s7, 256:260], ALU.add), g0[7 * g + 6])
            v = op(V, lambda e: e.scalar_tensor_tensor(out=A_, in0=B_, scalar=0.01, in1=B_, op0=ALU.mult, op1=ALU.max), v)
            v = op(V, lambda e: e.tensor_reduce(amx[:, s7], A_, AX.X, ALU.max), v)
            v = op(V, lambda e: e.tensor_tensor(B_, A_, bc(amx), ALU.subtract), v)
            v = op(S, lambda e: e.activation(A_, B_, ACT.Exp), v)
            v = op(V, lambda e: e.tensor_reduce(amx[:, s7], A_, AX.X, ALU.add), v)
            v = op(V, lambda e: e.reciprocal(degS[:, s7], amx[:, s7]), v)
            soft[g] = op(V, lambda e: e.tensor_tensor(B_, A_, bc(degS), ALU.mult), v)

        xt0 = use["pt"][NBK - 1]
        hfree = {}

        def res0(g, b):
            if b % 7 == 0:
                softmax(g)
            pr = ACC[:, b, 0:D].rearrange("p (h d) -> p h d", h=4)
            v = op(V, lambda e: e.tensor_tensor(
                pr, pr, alb[:, b, :].unsqueeze(2).to_broadcast([P, 4, 64]), ALU.mult), soft[g])
            h_ = hb[b % 3]
            v = op(V, lambda e: e.tensor_reduce(
                h_[:, 0:64], ACC[:, b, 0:D].rearrange("p (h d) -> p d h", h=4), AX.X, ALU.add), v,
                *([hfree[b - 3]] if b >= 3 else []))
            xv = X[:, b, :].rearrange("p (h d) -> p h d", h=4)
            hfree[b] = op(V, lambda e: e.tensor_tensor(
                xv, xv, h_[:, 0:64].unsqueeze(1).to_broadcast([P, 4, 64]), ALU.add), v, xt0)
            return hfree[b]

        regs = {}
        hist = {"gfree": [], "mfree": [], "afree": []}

        def aggregate(table, weighted, ready, width=D, background=None, share=0.0):
            gs, ms, mm_, adds = [], [], [], []
            credit = 0.0

            def add(k):
                if k % 4 == 0:
                    def ld(e, k=k):
                        h = (k // 4) % 2
                        if h not in regs:
                            regs[h] = [e.alloc_register(f"bk{h}_{i}") for i in range(4)]
                        e.load(regs[h], row[0:1, k:k + 4])
                        regs["v"] = [e.snap(r_, min_val=0, max_val=AW * (NBK - 1)) for r_ in regs[h]]
                    q.plain(V, ld, *ready)
                accf = ACC[:, :, :].rearrange("p b w -> p (b w)")

                def fn(e, k=k):
                    o = accf[:, bass.ds(regs["v"][k % 4], width)]
                    return e.tensor_tensor(o, o, PA[k % NA][:, 0:width], ALU.add)
                adds.append(op(V, fn, mm_[k], *adds[-1:]))
            for k in range(NCH):
                gf = [mm_[k - NG]] if k >= NG else hist["gfree"]
                gs.append(dma(G_, lambda e, k=k: e.indirect_dma_start(
                    G[k % NG][:, 0:D], None, table, bass.IndirectOffsetOnAxis(ap=idx[:, k:k + 1], axis=0)),
                    s_g[k % NG], *gf, *ready))
                mf = [mm_[k - NM]] if k >= NM else hist["mfree"]
                if weighted:
                    fn = lambda e, k=k: e.tensor_scalar(M[k % NM][:, :], iot[:, :], dlo[:, k:k + 1], wD[:, k:k + 1],
                                                        ALU.is_equal, ALU.mult)
                else:
                    fn = lambda e, k=k: e.tensor_scalar(M[k % NM][:, :], iot[:, :], dlo[:, k:k + 1], None, ALU.is_equal)
                ms.append(op(V, fn, *mf, *ready))
                af = [adds[k - NA]] if k >= NA else hist["afree"]
                wc = [op(S, lambda e, k=k: e.copy(G[k % NG][:, D:D + 1], wD[:, k:k + 1]), *gf, *ready)] if width > D else []
                mm_.append(op(T, lambda e, k=k: e.matmul(PA[k % NA][:, 0:width], M[k % NM][:, :], G[k % NG][:, 0:width],
                                                         start=True, stop=True), gs[k], ms[k], *wc, *af))
                credit += share
                while background is not None and credit > 0:
                    cost = next(background, None)
                    if cost is None:
                        background = None
                    else:
                        credit -= cost
                if k >= 2:
                    add(k - 2)
            add(NCH - 2)
            add(NCH - 1)
            assert background is None
            hist["gfree"], hist["mfree"], hist["afree"] = [mm_[-1]], [mm_[-1]], [adds[-1]]
            return adds[-1]

        def table_from(scale, TAB, Wt, wtok):
            toks = []

            def make(b, tok, src=None):
                src = X[:, b, :] if src is None else src

                def evac(ph, mt):
                    t = op(V, lambda e: e.tensor_scalar(ACC[:, b, 0:D], ph[:, 0:D], scale[:, b:b + 1], None, ALU.mult), mt)
                    r = rows_of(b)
                    toks.append(dma("sync", lambda e: e.dma_start(TAB[1 + b * P:1 + b * P + r, :], ACC[0:r, b, 0:D]),
                                    s_st[b % 2], t))
                    return t
                return project(src, Wt, D, [tok, *wtok], evac)
            return toks, make

        toks, then = table_from(d1, T1, W1, l_w)
        transition(res0, then, [k1])
        multiply()
        o2 = fb.op
        alld = [toks[-1], toks[-2], cps[-1], fl, k1]
        hk2 = split(keyi[0], [], [], op=o2)
        rF = {"base": rD["base"], "free": []}
        pay = scr[:, 0:2 * EC].rearrange("p (c o) -> p c o", o=2)
        adr = scr[:, 2 * EC:3 * EC].bitcast(I32)
        zf = o2(V, lambda e: e.memset(scr[:, 0:2 * NCH], 0.0))
        zd = load(SLOTD.rearrange("(p k) o -> p (k o)", p=P), scr[:, 0:2 * NCH], zf, queue=fb)
        finish(slots(rF, op=o2, after=hk2))
        o2(V, lambda e: e.tensor_copy(pay[:, :, 1], we[:, :]), zd, *l_we)
        v = o2(V, lambda e: e.tensor_copy(ti[:, :], rk[:, 0:EC]), rF["slots"])
        v = o2(V, lambda e: e.tensor_scalar(tj[:, :], ti[:, :], 127, None, ALU.bitwise_and), v)
        v = o2(V, lambda e: e.tensor_scalar(adr, ti[:, :], 7, None, ALU.logical_shift_right), v)
        v = o2(V, lambda e: e.scalar_tensor_tensor(out=ti[:, :], in0=tj[:, :], scalar=float(NCH), in1=adr,
                                                   op0=ALU.mult, op1=ALU.add), v)
        aD = o2(V, lambda e: e.tensor_copy(adr, ti[:, :]), v)
        v = o2(V, lambda e: e.tensor_scalar(rk[:, 0:EC], keyi[1][:, :], 1.0, 128.0, ALU.add, ALU.mult), aD, *l_src)
        pD = o2(V, lambda e: e.tensor_tensor(pay[:, :, 0], rk[:, 0:EC], lof[:, :], ALU.add), v)
        for c in range(EC):
            sD = fb.dma(G_, lambda e, c=c: e.indirect_dma_start(
                SLOTD, bass.IndirectOffsetOnAxis(ap=adr[:, c:c + 1].bitcast(U32), axis=0), pay[:, c, :], None,
                bounds_check=P * NCH - 1, oob_is_err=False), s_sD, aD, pD)
        l1 = load(scr[:, 0:2 * NCH], SLOTD.rearrange("(p k) o -> p (k o)", p=P), sD, queue=fb)
        slv = scr[:, 0:2 * NCH].rearrange("p (k o) -> p k o", o=2)
        idxi = idx[:, 0:NCH].bitcast(I32)
        v = o2(V, lambda e: e.tensor_copy(wD[:, 0:NCH], slv[:, :, 1]), l1)
        v = o2(V, lambda e: e.tensor_copy(idxi, slv[:, :, 0]))
        v = o2(V, lambda e: e.tensor_scalar(dlo[:, 0:NCH].bitcast(I32), idxi, 127, None, ALU.bitwise_and), v)
        v = o2(V, lambda e: e.tensor_copy(dlo[:, 0:NCH], dlo[:, 0:NCH].bitcast(I32)), v)
        v = o2(V, lambda e: e.tensor_scalar(idxi, idxi, 7, None, ALU.logical_shift_right), v)
        fb.plain(V, lambda e: None, v)
        q.branch((V, G_, "sync"), fb, flag[0:1, 0:1], *alld)
        l_row = [load(row[:, :], BKD[:, :], bkl)]
        zacc = op(V, lambda e: e.memset(ACC[:, :, 0:D + 1], 0.0), *toks[-2:])

        rS = {}

        def by_src():
            hs = split(keyi[1], l_src, [zacc])
            yield 2.0
            yield from chunk_map(rS, (PH[0], PH[1]), hs, [zacc, use["ph"][-1], use["ph"][-2], k1])
            rS["bk"] = load(BKS.rearrange("o (p t) -> (o p) t", t=7), bki[:, :], rS["bki"])
            yield from slots(rS)
            A_, B_, L_, K_ = (scr[:, i * 832:i * 832 + EC] for i in range(4))
            f = op(V, lambda e: e.tensor_scalar(sc[0][:, 0:EC], keyi[0][:, :], 1.0, 128.0, ALU.add, ALU.mult), rS["slots"])
            f = op(V, lambda e: e.tensor_tensor(A_, sc[0][:, 0:EC], lof[:, :], ALU.add), f)
            f = op(V, lambda e: e.tensor_copy(ti, A_), f)
            yield 2.0
            f = op(V, lambda e: e.tensor_scalar(tj, ti, 1023, None, ALU.bitwise_and), f)
            f = op(V, lambda e: e.tensor_copy(B_, tj), f)
            f = op(V, lambda e: e.tensor_scalar(tj, ti, 10, None, ALU.logical_shift_right), f)
            f = op(V, lambda e: e.tensor_copy(A_, tj), f)
            yield 2.5
            f = op(V, lambda e: e.tensor_copy(ti, rk[:, 0:EC]), f)
            f = op(V, lambda e: e.tensor_scalar(tj, ti, 127, None, ALU.bitwise_and), f)
            f = op(V, lambda e: e.tensor_copy(L_, tj), f)
            yield 2.5
            f = op(V, lambda e: e.tensor_scalar(tj, ti, 7, None, ALU.logical_shift_right), f)
            rS["pay"] = op(V, lambda e: e.tensor_copy(K_, tj), f)
            yield 2.0
            yield from degrees(rS, PH[0], [rS["base"], *hs])
            v = op(V, lambda e: e.tensor_scalar(degS[:, :], PH[0][:, 0:NBK], 1.0, None, ALU.add), rS["deg"])
            use["ph"] += [v] * 6
            use["pt"] += [use["pt"][-2], use["pt"][-1]] * 3
            use["xt"] += use["xt"][-3:] * 2
            rS["k3"] = rsqrt(d3, degS[:, :], ALL, v)()

        done = aggregate(T1, False, [*toks[-2:], *z_rows, *l_row, zacc], width=D + 1, background=by_src(), share=0.42)
        w_ = op(V, lambda e: e.tensor_scalar(degI[:, :], ACC[:, :, D], 1.0, None, ALU.add), done)
        v2 = op(V, lambda e: e.tensor_scalar(dk[:, :], degI[:, :], 0.0, None, ALU.is_gt), w_)
        v3_ = op(V, lambda e: e.tensor_scalar(degI[:, :], degI[:, :], 1e-30, None, ALU.max), v2)
        v3_ = rsqrt(d2, degI[:, :], ALL, v3_)()
        k2 = op(V, lambda e: e.tensor_tensor(d2[:, :], d2[:, :], dk[:, :], ALU.mult), v3_)

        def add_scaled(scale, done_):
            return lambda g, b: op(V, lambda e: e.scalar_tensor_tensor(
                out=X[:, b, :], in0=ACC[:, b, 0:D], scalar=scale[:, b:b + 1], in1=X[:, b, :],
                op0=ALU.mult, op1=ALU.add), done_)

        toks, then = table_from(d2, T2, W2, l_w)
        transition(add_scaled(d1, done), then, [k2])
        multiply()

        def permute(piece, out_):
            pv = scr[:, piece * 832:piece * 832 + EC]
            npv = rk[:, 0:EC]
            rS["n"] = op(V, lambda e: e.tensor_scalar(npv, pv, -1.0, None, ALU.mult), rS["pay"], rS.get("p0", rS["pay"]))
            L_, K_ = (scr[:, i * 832:i * 832 + EC] for i in (2, 3))
            oh = [big[i][:, 0:NCH] for i in range(2)]
            ol = [big[i][:, NCH:NCH + P] for i in range(2)]
            ab = M2
            rd, rl, mms = [], [], []
            w0 = [use["pt"][-1], use["pt"][-2], rS["pay"], rS["deg"], c_iok, rS["n"]]

            def products(c):
                op(T, lambda e: e.matmul(PT[0][:, 0:512], ol[c % 2], oh[c % 2][:, 0:512], start=c == 0, stop=c == EC - 1),
                   rd[c], rl[c])
                mms.append(op(T, lambda e: e.matmul(PT[1][:, 0:NCH - 512], ol[c % 2], oh[c % 2][:, 512:NCH],
                                                    start=c == 0, stop=c == EC - 1)))
            for c in range(EC):
                free = [mms[c - 2]] if c >= 2 else w0
                rd.append(op(V, lambda e, c=c: e.tensor_scalar(oh[c % 2], iok[:, 0:NCH], K_[:, c:c + 1], None,
                                                               ALU.is_equal), *free))
                v = op(S, lambda e, c=c: e.activation(ab[c % 2][:, :], iot[:, :], ACT.Abs, bias=L_[:, c:c + 1], scale=-1.0),
                       *(w0 if c < 2 else [rl[c - 2]]))
                rl.append(op(S, lambda e, c=c: e.activation(ol[c % 2], ab[c % 2][:, :], ACT.Relu, bias=pv[:, c:c + 1],
                                                            scale=npv[:, c:c + 1]), v, *free))
                if c >= 1:
                    products(c - 1)
                yield 1.0
            products(EC - 1)
            e1 = op(S, lambda e: e.copy(out_[:, 0:512], PT[0][:, 0:512]), mms[-1])
            e1 = op(S, lambda e: e.copy(out_[:, 512:NCH], PT[1][:, 0:NCH - 512]))
            rS[f"p{piece}"] = e1
            use["pt"] += [e1] * 6
            use["ph"] += [use["ph"][-2], use["ph"][-1]] * 3
            use["xt"] += use["xt"][-3:] * 2

        done = aggregate(T2, True, [*toks[-2:], *z_rows], background=permute(0, sc[0]), share=1.0)

        toks, then = table_from(d2, T3, W3, l_w)
        tr, hv = [], {}

        def hidden(b):
            h_ = hb[b % 3]
            v = op(V, lambda e: e.scalar_tensor_tensor(out=h_[:, :], in0=ACC[:, b, 0:D], scalar=d2[:, b:b + 1],
                                                       in1=b1[:, :], op0=ALU.mult, op1=ALU.add),
                   done, *l_b, *([tr[b - 3]] if b >= 3 else []))
            hv[b] = op(S, lambda e: e.activation(h_[:, :], h_[:, :], ACT.Relu), v)
        hidden(0)
        hidden(1)
        for b in range(NBK):
            if b + 2 < NBK:
                hidden(b + 2)
            tr.append(then(b, hv[b], hb[b % 3][:, :]))
        multiply()
        done = aggregate(T3, True, [*toks[-2:], *z_rows], background=permute(1, sc[1]), share=1.0)
        v = op(V, lambda e: e.scalar_tensor_tensor(out=rk[:, 0:NCH], in0=sc[0][:, 0:NCH], scalar=1024.0, in1=sc[1][:, 0:NCH],
                                                   op0=ALU.mult, op1=ALU.add), rS["p0"], rS["p1"])
        idxs = idx[:, 0:NCH].bitcast(I32)
        v = op(V, lambda e: e.tensor_copy(idxs, rk[:, 0:NCH]), v, done)
        v1 = op(V, lambda e: e.tensor_scalar(dlo[:, 0:NCH].bitcast(I32), idxs, 127, None, ALU.bitwise_and), v)
        v2 = op(V, lambda e: e.tensor_copy(dlo[:, 0:NCH], dlo[:, 0:NCH].bitcast(I32)), v1)
        v3_ = op(V, lambda e: e.tensor_scalar(idxs, idxs, 7, None, ALU.logical_shift_right), v1)
        rdS = [v2, v3_, load(row[:, :], BKS[:, :], rS["bk"], done)]

        def res2(g, b):
            h_ = hb[b % 3]
            v = op(V, lambda e: e.scalar_tensor_tensor(out=h_[:, :], in0=ACC[:, b, 0:D], scalar=d2[:, b:b + 1],
                                                       in1=b2[:, :], op0=ALU.mult, op1=ALU.add), done, tr[-1],
                   *([hv[("r", b - 3)]] if b >= 3 else []))
            hv[("r", b)] = op(V, lambda e: e.scalar_tensor_tensor(out=X[:, b, :], in0=h_[:, :], scalar=0.0, in1=X[:, b, :],
                                                                  op0=ALU.max, op1=ALU.add), v)
            return hv[("r", b)]
        for i in range(2):
            for j in range(2):
                t = op(T, lambda e, i=i, j=j: e.transpose(PA[i][:, j * P:(j + 1) * P], W4r[:, j, i * P:(i + 1) * P],
                                                          ident[:, :]), *l_w, *hist["afree"])
            wt = op(S, lambda e, i=i: e.copy(W4[:, i, 0:D], PA[i][:, 0:D]), t)
        hist["afree"] = hist["afree"] + [wt]
        toks, then = table_from(d3, T4, W4, [wt])
        transition(res2, then, [rS["k3"]])
        multiply()
        done = aggregate(T4, False, [*toks[-2:], *z_rows, *rdS])

        def store(b, tok):
            r = rows_of(b)
            dma("sync", lambda e: e.dma_start(out[b * P:b * P + r, :], X[0:r, b, :]), s_out, tok)
        transition(add_scaled(d3, done), store)
        q.plain("sync", lambda e: e.wait_ge(s_out, q.dma_n[s_out]), *l_we, *l_src, *l_pad)

        block = ctx.enter_context(nc.Block())
        block.sync(lambda e: q.run("sync", e))
        block.vector(lambda e: q.run("vector", e))
        block.scalar(lambda e: q.run("scalar", e))
        block.tensor(lambda e: q.run("tensor", e))
        block.gpsimd(lambda e: q.run("gpsimd", e))


def kernel(**inputs):
    import numpy as np
    import concourse.bacc as bacc
    from concourse.bass_utils import run_bass_kernel_spmd as run
    nc = bacc.Bacc("TRN2", target_bir_lowering=False, num_devices=1)
    arrays, args = {}, {}
    for name, v in inputs.items():
        v = np.ascontiguousarray(v)
        arrays[f"in_{name}"] = v
        args[name] = nc.dram_tensor(f"in_{name}", v.shape, mybir.dt.from_np(v.dtype), kind="ExternalInput").ap()
    out = nc.dram_tensor("out_0", (N, D), F32, kind="ExternalOutput").ap()
    program(nc, args, out)
    r = run(nc, [arrays], core_ids=[0])
    return r.results[0]["out_0"]
```

```python
from contextlib import ExitStack

import concourse.bass as bass
from concourse import mybir

F32 = mybir.dt.float32
BF16 = mybir.dt.bfloat16
I32 = mybir.dt.int32
U32 = mybir.dt.uint32
U16 = mybir.dt.uint16
ALU = mybir.AluOpType
ACT = mybir.ActivationFunctionType
AX = mybir.AxisListType

N, D, E = 6250, 256, 106250
P = 128
NBK = 49
LAST = N - (NBK - 1) * P
EC = 831
ETAIL = E - (P - 1) * EC
NCH = E // P + NBK + 1
KC = 896
PADN = (KC - E // P + 1) * P
AW = 264
EPS = 1e-5
NG, NM = 7, 4
NCF, PER_BLOCK, SLACK = 860, 17.5, 2.5
GROUPS = [0, 7, 14, 21, 28, 35, 42, 46, 49]
GROUP_OF = [sum(b >= g for g in GROUPS[1:]) for b in range(NBK)]
UNSLOTTED = float(127 + 128 * 1000)
F16 = mybir.dt.float16
T0_FIRST, MASK_FROM = 20, 38


class Queues:

    def __init__(self, sems):
        self.sem = sems
        self.n = {e: 0 for e in sems}
        self.dma_n = {}
        self.seen = {e: {} for e in list(sems) + ["sync"]}
        self.code = {e: [] for e in list(sems) + ["sync"]}

    def _waits(self, eng, waits):
        out = []
        for sem, val in waits:
            if self.seen[eng].get(sem, 0) < val:
                self.seen[eng][sem] = val
                out.append((sem, val))
        return out

    def op(self, eng, fn, *waits):
        self.n[eng] += 1
        self.code[eng].append((self._waits(eng, waits), fn, self.sem[eng], 1))
        return (self.sem[eng], self.n[eng])

    def dma(self, eng, fn, sem, *waits):
        self.dma_n[sem] = self.dma_n.get(sem, 0) + 16
        self.code[eng].append((self._waits(eng, waits), fn, sem, 16))
        return (sem, self.dma_n[sem])

    def plain(self, eng, fn, *waits):
        self.code[eng].append((self._waits(eng, waits), fn, None, 0))

    def branch(self, engines, inner, flag, *waits):
        for name in engines:
            def fn(eng, name=name):
                with eng.If(eng.value_load(flag, min_val=0, max_val=1) < 1):
                    inner.run(name, eng)
            self.plain(name, fn, *waits)

    def either(self, flag, versions, keep, *waits):
        before = (dict(self.n), dict(self.dma_n), {e: dict(v) for e, v in self.seen.items()})
        copy_ = lambda d: {k: list(v) if isinstance(v, list) else v for k, v in d.items()}
        kept = [copy_(d) for d in keep]
        whole, made = self.code, []
        for version in versions:
            self.n, self.dma_n = dict(before[0]), dict(before[1])
            self.seen = {e: dict(v) for e, v in before[2].items()}
            for d, k_ in zip(keep, kept):
                d.clear()
                d.update(copy_(k_))
            self.code = {e: [] for e in whole}
            version()
            made.append((self.n, self.dma_n, self.seen, self.code))
        (n0, m0, e0, _), (n1, m1, e1, _) = made
        self.n = {e: max(n0[e], n1[e]) for e in n0}
        for n_, _, _, code in made:
            for e in n_:
                rest = self.n[e] - n_[e]
                if rest:
                    at = max(i for i, c in enumerate(code[e]) if c[2] is self.sem[e])
                    w_, fn, sem_, by = code[e][at]
                    code[e][at] = (w_, fn, sem_, by + rest)
        self.dma_n = {**m0, **m1}
        assert all(m0[s_] == m1[s_] for s_ in m0 if s_ in m1)
        self.seen = {e: {s_: min(v, e1[e].get(s_, 0)) for s_, v in e0[e].items()} for e in e0}
        last = {self.sem[e]: self.n[e] for e in self.n}

        def settle(x):
            if isinstance(x, list):
                return [settle(y) for y in x]
            if isinstance(x, tuple) and len(x) == 2 and x[0] in last and x[1] > before[0][by_sem[x[0]]]:
                return (x[0], last[x[0]])
            return x
        by_sem = {self.sem[e]: e for e in self.n}
        for d in keep:
            for k_ in d:
                d[k_] = settle(d[k_])
        self.code = whole
        for name in whole:
            def fn(eng, name=name):
                with eng.If(eng.value_load(flag, min_val=0, max_val=1) < 1):
                    self.play(made[0][3][name], eng)
                with eng.Else():
                    self.play(made[1][3][name], eng)
            self.plain(name, fn, *waits)

    def run(self, name, eng):
        self.play(self.code[name], eng)

    def play(self, code, eng):
        for waits, fn, sem, by in code:
            for s, v in waits:
                eng.wait_ge(s, v)
            ins = fn(eng)
            if sem is not None:
                ins.then_inc(sem, by)


def program(nc, a, out):
    dr = lambda n, s, d=F32: nc.dram_tensor(n, s, d, kind="Internal").ap()
    T0, T1, T2, T3, T4 = (dr("T0", (N, 260)), dr("T1", (N + 1, D)), dr("T2", (N + 1, D)),
                          dr("T3", (N + 1, D)), dr("T4", (N + 1, D)))
    TL = dr("TL", (N, 4))
    SLOTD = dr("SLOTD", (P * NCH, 2))
    LD, LS, LW = dr("LD", (E + PADN, 1), I32), dr("LS", (E + PADN, 1), I32), dr("LW", (E + PADN, 1))
    BKD, BKS = dr("BKD", (1, KC), I32), dr("BKS", (1, KC), I32)
    with ExitStack() as ctx:
        sb = lambda n, s, d=F32: ctx.enter_context(nc.sbuf_tensor(n, s, d))
        sem = lambda n: ctx.enter_context(nc.semaphore(n))
        X = sb("X", [P, NBK, D])
        ACC = sb("ACC", [P, NBK, AW])
        iot = sb("iot", [P, P])
        pid = sb("pid", [P, 1])
        ident = sb("ident", [P, P])
        lower = sb("lower", [P, P])
        ones = sb("ones", [P, P])
        kio = sb("kio", [P, 7])
        irep = sb("irep", [P, P, 8], F16)
        iok = sb("iok", [P, KC], F16)
        W0 = sb("W0", [P, 2, AW])
        W1, W2, W3, W4r = (sb(f"Wt{i}", [P, 2, D]) for i in range(4))
        W4 = W0
        b1, b2 = (sb(f"bc{i}", [P, D]) for i in range(2))
        hb = [sb(f"hb{i}", [P, D]) for i in range(3)]
        atl, atr, wtmp = hb
        keyi = [sb(f"keyi{i}", [P, EC], I32) for i in range(2)]
        we = sb("we", [P, EC])
        hi = sb("hi", [P, EC], F16)
        lof = sb("lof", [P, EC], F16)
        zb = sb("zb", [P, EC], BF16)
        mm = [sb(f"mm{i}", [P, EC], BF16) for i in range(2)]
        sc = [sb(f"sc{i}", [P, KC]) for i in range(2)]
        ti, tj = (t_[:, 0:EC].bitcast(I32) for t_ in sc)
        rk = sb("rk", [P, KC])
        cnt = sb("cnt", [P, NBK])
        s49 = [sb(f"s49{i}", [P, NBK]) for i in range(5)]
        i49 = [sb(f"i49{i}", [P, NBK], I32) for i in range(2)]
        bks7, bkst = sb("bks7", [P, 7]), sb("bkst", [P, 7])
        bki = sb("bki", [P, 7], I32)
        sti = sb("sti", [P, 7], I32)
        scr = sb("scr", [P, 4 * 832])
        big = [sb(f"big{i}", [P, 8 * (P + NBK)], F16) for i in range(3)]
        wD = sb("wD", [P, KC])
        idx = sb("idx", [P, KC], U32)
        dlo = sb("dlo", [P, KC])
        row = sb("row", [1, KC], I32)
        flag = sb("flag", [1, 1], I32)
        srcN = sb("srcN", [P, NBK], I32)
        dstN = sb("dstN", [P, NBK], I32)
        degI, degS = sb("degI", [P, NBK]), sb("degS", [P, NBK])
        d1, d2, d3, dk = (sb(f"d{i}", [P, NBK]) for i in range(4))
        vpe = sb("vpe", [P, NBK])
        late_, okD, okS = sb("late", [P, 1]), sb("okD", [1, 1], I32), sb("okS", [1, 1], I32)
        G = [sb(f"G{i}", [P, D + 1]) for i in range(NG)]
        M = [sb(f"M{i}", [P, P]) for i in range(NM)]
        xT = [sb(f"xT{i}", [P, 2, P]) for i in range(3)]
        M2 = [sb(f"M2{i}", [P, P]) for i in range(2)]
        st = sb("st", [P, NBK, 6])
        mv = sb("mv", [P, NBK, 2])
        rstd, nmr = sb("rstd", [P, NBK]), sb("nmr", [P, NBK])
        rq, rqs = ([sb(f"{n_}{i}", [P, NBK]) for i in range(4)] for n_ in ("rq", "rqs"))
        al = sb("al", [P, NBK, 4])
        alb = sb("alb", [P, NBK, 4])
        amx = sb("amx", [P, NBK])
        tot = sb("tot", [P, 1])
        PA = [ctx.enter_context(nc.psum_tensor(f"PA{i}", [P, 512], F32)) for i in range(4)]
        PT = [ctx.enter_context(nc.psum_tensor(f"PT{i}", [P, 512], F32)) for i in range(2)]
        PH = [ctx.enter_context(nc.psum_tensor(f"PH{i}", [P, 512], F32)) for i in range(2)]
        q = Queues({e: sem(f"s_{e}") for e in ("vector", "scalar", "tensor", "gpsimd")})
        fb = Queues({e: sem(f"f_{e}") for e in ("vector", "scalar", "tensor", "gpsimd")})
        op, dma = q.op, q.dma
        V, S, T, G_ = "vector", "scalar", "tensor", "gpsimd"
        s_st = [sem(f"s_st{i}") for i in range(2)]
        s_sD, s_out, s_sl = sem("s_sD"), sem("s_out"), sem("s_sl")
        s_l0 = [sem(f"s_l0{i}") for i in range(len(GROUPS) - 1)]
        ndma = [0]

        sems_ = {}

        def by_name(n_):
            if n_ not in sems_:
                sems_[n_] = sem(n_)
            return sems_[n_]

        def load(dst, src, *waits, eng="sync", slow=False, queue=None):
            ndma[0] += 1
            return (queue or q).dma(eng, lambda e: e.dma_start(dst, src, allow_slow_non_contiguous=slow),
                                    by_name(f"s_ld{ndma[0]}"), *waits)

        def rsqrt(dst, src, sl, tok, rq=rq):
            r = [t_[:, sl] for t_ in rq]
            root = op(S, lambda e: e.activation(r[0], src, ACT.Sqrt), tok)
            parts = [
                lambda t: op(V, lambda e: e.reciprocal(r[1], r[0]), root),
                lambda t: op(V, lambda e: e.tensor_tensor(r[2], r[1], r[1], ALU.mult), t),
                lambda t: op(V, lambda e: e.scalar_tensor_tensor(out=r[3], in0=src, scalar=-0.5, in1=r[2],
                                                                 op0=ALU.mult, op1=ALU.mult), t),
                lambda t: op(V, lambda e: e.scalar_tensor_tensor(out=dst[:, sl], in0=r[3], scalar=1.5, in1=r[1],
                                                                 op0=ALU.add, op1=ALU.mult), t)]
            return lambda t: parts.pop(0)(t)

        def rsqrt_all(dst, src, tok, rq=rq):
            part, t = rsqrt(dst, src, slice(0, NBK), tok, rq), None
            for _ in range(4):
                t = part(t)
            return t

        io = lambda t_, pat, cm: op(G_, lambda e: e.iota(t_, pat, base=0, channel_multiplier=cm,
                                                         allow_small_or_imprecise_dtypes=True))
        c_iot = io(iot[:, :], [[1, P]], 0)
        c_pid = io(pid[:, :], [[1, 1]], 1)
        c_kio = io(kio[:, :], [[1, 7]], 7)
        c_rep = io(irep[:, :, :], [[1, P], [0, 8]], 0)
        c_iok = io(iok[:, :], [[1, KC]], 0)
        z_key = [op(V, lambda e, i=i: e.memset(keyi[i][96:128, ETAIL:EC], 8192)) for i in range(2)]
        z_idx = op(V, lambda e: e.memset(srcN[:, NBK - 1:NBK], 0))
        z_idx = op(V, lambda e: e.memset(dstN[:, NBK - 1:NBK], 0))
        z_we = op(V, lambda e: e.memset(we[96:128, ETAIL:EC], 0.0))
        z_x = op(V, lambda e: e.memset(X[96:128, NBK - 1, :], 0.0))
        z_p1 = op(V, lambda e: e.memset(dlo[:, 0:PADN // P].bitcast(I32), 8192))
        z_p0 = op(V, lambda e: e.memset(wD[:, 0:256], 0.0))
        c_zb = op(V, lambda e: e.memset(zb[:, :], 0.0))
        c_on = op(V, lambda e: e.memset(ones[:, :], 1.0))

        def load_edges(dst, src, z):
            return [load(dst[0:112, :], src[0:112 * EC].rearrange("(p c) -> p c", c=EC), z),
                    load(dst[112:127, :], src[112 * EC:127 * EC].rearrange("(p c) -> p c", c=EC), z),
                    load(dst[127:128, 0:ETAIL], src[127 * EC:E].rearrange("(p c) -> p c", p=1), z)]

        l_w0 = load(W0[:, :, 0:D], a["L0_gnn_weight"].rearrange("(t p) d -> p t d", p=P), eng=S)
        l_dst = load_edges(keyi[0], a["dst"], z_key[0])
        l_at = [load(t_[:, :], a[n_].rearrange("(o h) d -> o (h d)", o=1).to_broadcast([P, D]), eng=S)
                for t_, n_ in ((atl, "L0_gnn_attn_l"), (atr, "L0_gnn_attn_r"))]
        l_x = [load(X[:, 6 * i:6 * i + 6, :], a["x"][6 * i * P:(6 * i + 6) * P, :].rearrange("(b p) d -> p b d", p=P))
               for i in range(8)] + [load(X[0:LAST, 48, :], a["x"][48 * P:N, :], z_x)]
        l_pad = []
        for t_, n_, pad, z in ((LD, "dst", dlo[:, 0:PADN // P].bitcast(I32), z_p1),
                               (LS, "src", wD[:, 0:PADN // P].bitcast(I32), z_p0),
                               (LW, "edge_weight", wD[:, 0:PADN // P], z_p0)):
            l_pad.append(load(t_[0:E, :].rearrange("(p c) o -> p (c o)", p=125),
                              a[n_].rearrange("(p c) -> p c", p=125), eng=S))
            l_pad.append(load(t_[E:E + PADN, :].rearrange("(p c) o -> p (c o)", p=P), pad, z, eng=S))
        l_nodes = []
        for t_, n_ in ((srcN, "src"), (dstN, "dst")):
            l_nodes.append(load(t_[:, 0:48], a[n_][0:48 * P].rearrange("(b p) -> p b", p=P), slow=True))
            l_nodes.append(load(t_[0:LAST, 48:49], a[n_][48 * P:N].rearrange("(p o) -> p o", o=1), z_idx, slow=True))
        l_src = load_edges(keyi[1], a["src"], z_key[1])
        l_we = load_edges(we, a["edge_weight"], z_we)
        l_w = [load(t_[:, :, :], a[n_].rearrange("(t p) d -> p t d", p=P), eng=S)
               for t_, n_ in ((W1, "L1_gnn_W"), (W2, "L2_gnn_W1"), (W3, "L2_gnn_W2"), (W4r, "L3_gnn_W"))]
        l_b = [load(t_[:, :], a[n_].rearrange("(o d) -> o d", o=1).to_broadcast([P, D]), eng=S)
               for t_, n_ in ((b1, "L2_gnn_b1"), (b2, "L2_gnn_b2"))]
        z_rows = [load(t_[0:1, :], wD[0:1, 0:D], z_p0, eng=S) for t_ in (T1, T2, T3, T4)]

        c_id = op(V, lambda e: e.tensor_scalar(ident[:, :], iot[:, :], pid[:, 0:1], None, ALU.is_equal), c_pid, c_iot)
        c_lo = op(V, lambda e: e.tensor_scalar(lower[:, :], iot[:, :], pid[:, 0:1], None, ALU.is_gt))

        wa = []
        for t in range(2):
            for col, at in ((256, atr), (260, atl)):
                m_ = op(V, lambda e, t=t, at=at: e.tensor_tensor(wtmp[:, :], W0[:, t, 0:D], at[:, :], ALU.mult),
                        l_w0, *l_at, *wa)
                wa = [op(V, lambda e, t=t, col=col: e.tensor_reduce(
                    W0[:, t, col:col + 4], wtmp[:, :].rearrange("p (h d) -> p h d", h=4), AX.X, ALU.add), m_)]

        use = {"pt": [], "ph": [], "xt": [], "tr": []}
        held = []

        def multiply():
            xt, ph, Wt, width, cp, evac = held.pop(0)
            n = len(use["ph"])
            w_ph = [use["ph"][n - 2]] if n >= 2 else []
            for t in range(2):
                mt = op(T, lambda e, t=t: e.matmul(ph[:, 0:width], xt[:, t, :], Wt[:, t, 0:width],
                                                  start=t == 0, stop=t == 1), cp, *w_ph)
            use["xt"].append(mt)
            use["ph"].append(evac(ph, mt))

        def project(src_ap, Wt, width, ready, evac):
            n = len(use["pt"])
            pt, ph, xt = PT[n % 2], PH[n % 2], xT[n % 3]
            w_pt = [use["pt"][n - 2]] if n >= 2 else []
            op(T, lambda e: e.transpose(pt[:, 0:P], src_ap[:, 0:P], ident[:, :]), c_id, *ready, *w_pt)
            tr = op(T, lambda e: e.transpose(pt[:, P:2 * P], src_ap[:, P:2 * P], ident[:, :]))
            w_xt = [use["xt"][n - 3]] if n >= 3 else []
            cp = op(S, lambda e: e.copy(xt[:, :, :].rearrange("p t n -> p (t n)"), pt[:, 0:2 * P]), tr, *w_xt)
            use["pt"].append(cp)
            use["tr"].append(tr)
            if held:
                multiply()
            held.append((xt, ph, Wt, width, cp, evac))
            return tr

        def rows_of(b):
            return LAST if b == NBK - 1 else P

        def split(key, lk, guard, op=op):
            t = op(V, lambda e: e.tensor_scalar(ti[:, :], key[:, :], 7, None, ALU.logical_shift_right), *lk, *guard)
            t1 = op(V, lambda e: e.tensor_copy(hi[:, :], ti[:, :]), t)
            t2 = op(V, lambda e: e.tensor_scalar(tj[:, :], key[:, :], 127, None, ALU.bitwise_and))
            return [t1, op(V, lambda e: e.tensor_copy(lof[:, :], tj[:, :]), t2)]

        def chunk_map(res, banks, key_tok, guard, ok, op=op, starts=False):
            b0, b1_ = banks
            counts = []
            for b in range(NBK):
                w_ = [counts[b - 2]] if b >= 2 else []
                counts.append(op(V, lambda e, b=b: e.tensor_scalar(
                    mm[b % 2][:, :], hi[:, :], float(b), 0.0, ALU.is_equal, ALU.add, accum_out=cnt[:, b:b + 1]),
                    *key_tok, *w_, *guard))
                yield 0.5
            p1 = op(T, lambda e: e.matmul(b0[:, 0:NBK], lower[:, :], cnt[:, :], start=True, stop=True), counts[-1], c_lo, *guard)
            p2 = op(T, lambda e: e.matmul(b1_[:, 0:NBK], ones[:, :], cnt[:, :], start=True, stop=True), c_on)
            v = op(V, lambda e: e.tensor_scalar(i49[0][:, :], b1_[:, 0:NBK], 127.0, None, ALU.add), p2)
            v = op(V, lambda e: e.tensor_scalar(i49[1][:, :], i49[0][:, :], 7, None, ALU.logical_shift_right), v)
            v = op(V, lambda e: e.tensor_copy(s49[0][:, :], i49[1][:, :]), v)
            incl = op(V, lambda e: e.tensor_tensor_scan(s49[1][:, :], s49[0][:, :], zb[:, 0:NBK], 0.0, ALU.add, ALU.add), v, c_zb)
            v = op(V, lambda e: e.tensor_tensor(s49[2][:, :], s49[1][:, :], s49[0][:, :], ALU.subtract), incl)
            v = op(V, lambda e: e.tensor_scalar(s49[3][:, :], s49[2][:, :], 128.0, -1.0, ALU.mult, ALU.add), v)
            res["base"] = op(V, lambda e: e.tensor_tensor(s49[4][:, :], b0[:, 0:NBK], s49[3][:, :], ALU.add), v, p1)
            u = op(V, lambda e: e.scalar_tensor_tensor(out=cnt[:, :], in0=iot[:, 0:NBK], scalar=-PER_BLOCK, in1=s49[1][:, :],
                                                       op0=ALU.mult, op1=ALU.add), incl, p1, p2)
            u = op(V, lambda e: e.tensor_reduce(late_[:, :], cnt[:, :], AX.X, ALU.max), u)
            res["ok"] = op(V, lambda e: e.tensor_scalar(ok[:, :], late_[0:1, :], PER_BLOCK + SLACK, None, ALU.is_le), u)
            yield 2.0
            le = rk[:, 0:7 * NBK].rearrange("p (t b) -> p t b", t=7)
            u = op(V, lambda e: e.tensor_tensor(
                le, s49[1][:, :].unsqueeze(1).to_broadcast([P, 7, NBK]),
                kio[:, :].unsqueeze(2).to_broadcast([P, 7, NBK]), ALU.is_le), incl, c_kio)
            bt = op(V, lambda e: e.tensor_reduce(bks7[:, :], le, AX.X, ALU.add), u)
            u = op(V, lambda e: e.tensor_scalar(bki[:, :], bks7[:, :], float(NBK - 1), float(AW), ALU.min, ALU.mult), bt)
            res["bki"] = u
            if starts:
                v = op(V, lambda e: e.scalar_tensor_tensor(out=s49[2][:, :], in0=s49[0][:, :], scalar=-128.0,
                                                           in1=b1_[:, 0:NBK], op0=ALU.mult, op1=ALU.add), v)
                v = op(V, lambda e: e.tensor_tensor(le, le, s49[2][:, :].unsqueeze(1).to_broadcast([P, 7, NBK]), ALU.mult),
                       v, bt)
                v = op(V, lambda e: e.tensor_reduce(bkst[:, :], le, AX.X, ALU.add), v)
                v = op(V, lambda e: e.scalar_tensor_tensor(out=sti[:, :], in0=kio[:, :], scalar=128.0, in1=bkst[:, :],
                                                           op0=ALU.mult, op1=ALU.add), v)
                res["starts"] = v
            res["free"] = [u, v, p2]
            yield 1.5

        def slots(res, op=op, after=[]):
            r0 = op(V, lambda e: e.memset(rk[:, :], UNSLOTTED), *res["free"], *after)
            prev = []
            for b in range(NBK):
                m_ = op(V, lambda e, b=b: e.tensor_scalar(mm[b % 2][:, :], hi[:, :], float(b), None, ALU.is_equal),
                        *(res["free"] if b == 0 else []), *prev[-2:-1], *after)
                yield 0.6
                s_ = op(V, lambda e, b=b: e.tensor_tensor_scan(sc[b % 2][:, 0:EC], mm[b % 2][:, :], zb[:, :],
                                                              s49[4][:, b:b + 1], ALU.add, ALU.add), m_, res["base"], *after)
                yield 1.2
                prev.append(op(V, lambda e, b=b: e.copy_predicated(rk[:, 0:EC], mm[b % 2][:, :].bitcast(U16),
                                                                  sc[b % 2][:, 0:EC]), s_, r0, *prev[-1:]))
                yield 1.2
            res["slots"] = prev[-1]

        def degrees(res, bank, after, lag=1):
            groups, mms = [], []

            def products(n):
                x2, ol, oh, c0, g = groups[n]
                for i in range(g):
                    c = c0 + i
                    m_ = op(T, lambda e, ol=ol, oh=oh, i=i, c=c: e.matmul(
                        bank[:, 0:NBK], ol[:, :, i], oh[:, :, i], start=c == 0, stop=c == EC - 1), x2, *after)
                mms.append(m_)
            for n, c0 in enumerate(range(0, EC, 8)):
                g = min(8, EC - c0)
                B = big[n % 2]
                ol = B[:, 0:g * P].rearrange("p (j g) -> p j g", g=g)
                oh = B[:, 8 * P:8 * P + g * NBK].rearrange("p (j g) -> p j g", g=g)
                free = [mms[n - 2]] if n >= 2 else []
                op(V, lambda e, ol=ol, c0=c0, g=g: e.tensor_tensor(
                    ol, irep[:, :, 0:g], lof[:, c0:c0 + g].unsqueeze(1).to_broadcast([P, P, g]), ALU.is_equal),
                    *free, *after, c_rep)
                x2 = op(V, lambda e, oh=oh, c0=c0, g=g: e.tensor_tensor(
                    oh, irep[:, 0:NBK, 0:g], hi[:, c0:c0 + g].unsqueeze(1).to_broadcast([P, NBK, g]), ALU.is_equal))
                groups.append((x2, ol, oh, c0, g))
                if n >= lag:
                    products(n - lag)
                yield 0.95
            for n in range(len(groups) - lag, len(groups)):
                products(n)
            res["deg"] = mms[-1]

        def finish(gen):
            for _ in gen:
                pass

        t0_st = {}

        def t0_block(b):
            r = rows_of(b)

            def evac(ph, mt):
                t = op(S, lambda e: e.copy(ACC[:, b, 0:264], ph[:, 0:264]), mt)
                t0_st[0] = dma("sync", lambda e: e.dma_start(T0[b * P:b * P + r, :], ACC[0:r, b, 0:260]), s_st[0], t)
                t0_st[1] = dma("sync", lambda e: e.dma_start(TL[b * P:b * P + r, :], ACC[0:r, b, 260:264]), s_st[1], t)
                return t
            project(X[:, b, :], W0, 264, [l_x[b // 6], *wa], evac)

        for b in range(T0_FIRST):
            t0_block(b)
        hk = split(keyi[0], l_dst, [])
        rD = {}
        finish(chunk_map(rD, (PA[0], PA[1]), hk, [], okD, starts=True))
        KD, KS = (scr[:, i * KC:(i + 1) * KC].bitcast(I32) for i in range(2))
        KW = scr[:, 2 * KC:3 * KC]
        sl = []
        for t_, dram, i32 in ((KD, LD, 1), (KS, LS, 1), (KW, LW, 0)):
            for t in range(7):
                s_ = dma(G_, lambda e, t_=t_, dram=dram, t=t: e.indirect_dma_start(
                    t_[:, t * P:(t + 1) * P], None, dram,
                    bass.IndirectOffsetOnAxis(ap=sti[:, t:t + 1].bitcast(U32), axis=0)), s_sl, rD["starts"], *l_pad)
        def masked():
            bt7 = bks7[:, :].unsqueeze(2).to_broadcast([P, 7, P])
            v3 = lambda t_: t_.rearrange("p (t n) -> p t n", t=7)
            v = op(V, lambda e: e.tensor_scalar(scf[0].bitcast(I32), KD, 7, None, ALU.logical_shift_right), s_, *hk)
            yield
            v = op(V, lambda e: e.tensor_copy(scf[1], scf[0].bitcast(I32)), v)
            yield
            msk = op(V, lambda e: e.tensor_tensor(v3(rk[:, :]), v3(scf[1]), bt7, ALU.is_equal), v, *rD["free"])
            yield
            ms_["val"] = op(V, lambda e: e.scalar_tensor_tensor(out=scf[0], in0=KS, scalar=1.0, in1=rk[:, :],
                                                                op0=ALU.add, op1=ALU.mult), msk)
            yield
            ms_["wv"] = op(V, lambda e: e.tensor_tensor(KW, KW, rk[:, :], ALU.mult), msk)
            yield
            ms_["tt"] = op(V, lambda e: e.tensor_reduce(tot[:, :], rk[:, :], AX.X, ALU.add), msk)
            yield
            v = op(V, lambda e: e.tensor_scalar(KD, KD, 127, None, ALU.bitwise_and))
            yield
            ms_["lv"] = op(V, lambda e: e.tensor_copy(scf[1], KD), v, msk)
            yield

        scf = [t_[:, :] for t_ in sc]
        ms_ = {}
        msk_ = masked()
        deg = degrees(rD, PA[3], hk)
        for b in range(T0_FIRST, NBK):
            t0_block(b)
            next(deg)
            if b >= MASK_FROM:
                next(msk_, None)
        multiply()
        finish(msk_)
        t0_done = [t0_st[0], t0_st[1]]
        g0 = []
        for b in range(NBK):
            dma(G_, lambda e, b=b: e.indirect_dma_start(
                ACC[:, b, 0:260], None, T0, bass.IndirectOffsetOnAxis(ap=dstN[:, b:b + 1].bitcast(U32), axis=0)),
                s_l0[GROUP_OF[b]], *t0_done, *l_nodes)
            g0.append(dma(G_, lambda e, b=b: e.indirect_dma_start(
                al[:, b, :], None, TL, bass.IndirectOffsetOnAxis(ap=srcN[:, b:b + 1].bitcast(U32), axis=0)),
                s_l0[GROUP_OF[b]], *t0_done, *l_nodes))

        finish(deg)
        v = op(V, lambda e: e.tensor_copy(degI[:, :], PA[3][:, 0:NBK]), rD["deg"])
        v2 = op(V, lambda e: e.tensor_scalar(dk[:, :], degI[:, :], 0.0, None, ALU.is_gt), v)
        v = op(V, lambda e: e.tensor_scalar(degI[:, :], degI[:, :], 1.0, None, ALU.max), v2)
        v = rsqrt_all(d1, degI[:, :], v)
        k1 = op(V, lambda e: e.tensor_tensor(d1[:, :], d1[:, :], dk[:, :], ALU.mult), v2, v)

        val, wv, lv, tt = (ms_[n_] for n_ in ("val", "wv", "lv", "tt"))
        pt_ = op(T, lambda e: e.matmul(PA[0][:, 0:1], ones[:, :], tot[:, :], start=True, stop=True), tt, rD["base"])
        fl = op(V, lambda e: e.tensor_scalar(flag[:, :], PA[0][0:1, 0:1], float(E), None, ALU.is_equal), pt_)
        l_row = []
        bkl = load(BKD.rearrange("o (p t) -> (o p) t", t=7), bki[:, :], rD["bki"])
        cps = []
        for i, (src_, dst_, tk) in enumerate(((scf[0], idx[:, :], val), (scf[1], dlo[:, :], lv), (KW, wD[:, :], wv))):
            for h, (ta, tb) in enumerate(((0, 4), (4, 7))):
                bank = PA[(2 * i + h) % 3 + 1]
                g_ = [cps[2 * i + h - 3]] if 2 * i + h >= 3 else [rD["free"][1], k1]
                for t in range(ta, tb):
                    tr = op(T, lambda e, t=t, ta=ta, bank=bank, src_=src_: e.transpose(
                        bank[:, (t - ta) * P:(t - ta + 1) * P], src_[:, t * P:(t + 1) * P], ident[:, :]), tk, *g_)
                dv = dst_.rearrange("p (k t) -> p t k", t=7)[:, ta:tb, :]
                cps.append(op(V, lambda e, dv=dv, bank=bank, ta=ta, tb=tb: e.tensor_copy(
                    dv, bank[:, 0:(tb - ta) * P].rearrange("p (t k) -> p t k", k=P)), tr, *l_pad, *z_rows))
        def transition(stages, then, before=None):
            stages = stages + [
                lambda b, tok: op(V, lambda e: e.bn_stats(st[:, b, :], X[:, b, :]), tok),
                lambda b, tok: op(V, lambda e: e.bn_aggr(mv[:, b, :], st[:, b, :]), tok)]
            small, ready, tok = [], [], {}

            def tiny():
                if small:
                    small.pop(0)()

            def normalize(g, stt):
                sg = slice(GROUPS[g], GROUPS[g + 1])
                h = {}

                def first():
                    t = op(V, lambda e: e.tensor_scalar(vpe[:, sg], mv[:, sg, 1], EPS, None, ALU.add), stt)
                    h["parts"] = rsqrt(rstd, vpe[:, sg], sg, t)

                def last():
                    t = op(V, lambda e: e.scalar_tensor_tensor(out=nmr[:, sg], in0=mv[:, sg, 0], scalar=-1.0,
                                                               in1=rstd[:, sg], op0=ALU.mult, op1=ALU.mult), h["t"])
                    small[:0] = [lambda b=b: apply(b, t) for b in range(GROUPS[g], GROUPS[g + 1])]

                def apply(b, t):
                    ready.append((b, op(S, lambda e: e.activation(
                        X[:, b, :], X[:, b, :], ACT.Identity, bias=nmr[:, b:b + 1], scale=rstd[:, b:b + 1]), t)))

                def part():
                    h["t"] = h["parts"](h.get("t"))
                small.extend([first, lambda: None, part, part, part, part, last])
            done_ = 0
            step = 0
            while done_ < NBK:
                if before is not None:
                    for g in range(len(GROUPS) - 1):
                        if step == before[1](g):
                            small.extend(before[0](g))
                for j in reversed(range(len(stages))):
                    b = step - j
                    if 0 <= b < NBK:
                        yield min(step, NBK - 1)
                        tok[b] = stages[j](b, tok.get(b))
                        tiny()
                        if j == len(stages) - 1 and b + 1 in GROUPS:
                            normalize(GROUP_OF[b], tok[b])
                if len(ready) > 1 or ready and (not small or step >= NBK):
                    yield min(step, NBK - 1)
                    then(*ready.pop(0))
                    done_ += 1
                tiny()
                if step >= NBK:
                    tiny()
                    tiny()
                step += 1

        soft = {}

        def softmax(g):
            s7 = slice(GROUPS[g], GROUPS[g + 1])
            n7 = GROUPS[g + 1] - GROUPS[g]
            A_, B_ = al[:, s7, :], alb[:, s7, :]
            bc = lambda t_: t_[:, s7].unsqueeze(2).to_broadcast([P, n7, 4])
            h = {"t": g0[GROUPS[g + 1] - 1]}

            def nxt(eng, fn):
                def do():
                    h["t"] = soft[g] = op(eng, fn, h["t"])
                return do
            return [
                nxt(V, lambda e: e.tensor_tensor(B_, A_, ACC[:, s7, 256:260], ALU.add)),
                nxt(V, lambda e: e.scalar_tensor_tensor(out=A_, in0=B_, scalar=0.01, in1=B_, op0=ALU.mult, op1=ALU.max)),
                nxt(V, lambda e: e.tensor_reduce(amx[:, s7], A_, AX.X, ALU.max)),
                nxt(V, lambda e: e.tensor_tensor(B_, A_, bc(amx), ALU.subtract)),
                nxt(S, lambda e: e.activation(A_, B_, ACT.Exp)),
                nxt(V, lambda e: e.tensor_reduce(amx[:, s7], A_, AX.X, ALU.add)),
                nxt(V, lambda e: e.reciprocal(degS[:, s7], amx[:, s7])),
                nxt(V, lambda e: e.tensor_tensor(B_, A_, bc(degS), ALU.mult))]

        xt0 = use["pt"][NBK - 1]
        hfree = {}
        heads = lambda t_: t_.rearrange("p (h d) -> p h d", h=4)
        mix = [
            lambda b, tok: op(V, lambda e: e.tensor_tensor(
                heads(ACC[:, b, 0:D]), heads(ACC[:, b, 0:D]), alb[:, b, :].unsqueeze(2).to_broadcast([P, 4, 64]),
                ALU.mult), soft[GROUP_OF[b]]),
            lambda b, tok: op(V, lambda e: e.tensor_reduce(
                hb[b % 3][:, 0:64], ACC[:, b, 0:D].rearrange("p (h d) -> p d h", h=4), AX.X, ALU.add), tok,
                *([hfree[b - 3]] if b >= 3 else []))]

        zeroed = {}

        def clear(b, tok):
            zeroed[0] = op(S, lambda e: e.copy(ACC[:, b, 0:D + 1], zb[:, 0:D + 1]), tok)

        def spread(b, tok):
            hfree[b] = op(V, lambda e: e.tensor_tensor(
                heads(X[:, b, :]), heads(X[:, b, :]), hb[b % 3][:, 0:64].unsqueeze(1).to_broadcast([P, 4, 64]), ALU.add),
                tok, xt0)
            clear(b, tok)
            return hfree[b]

        regs = {}
        hist = {"gfree": [], "mfree": [], "afree": []}
        npass = [0]

        def aggregate(table, weighted, ready, banks, width=D, background=None, share=0.0, chunks=NCH, units=None):
            gs, ms, mm_, adds = [], [], [], []
            credit = 0.0
            na = len(banks)
            s_g = [by_name(f"s_g{npass[0]}_{chunks}_{i}") for i in range(NG)]
            need = None if units is None else next(units)

            def add(k):
                if k % 4 == 0:
                    def ld(e, k=k):
                        h = (k // 4) % 2
                        if h not in regs:
                            regs[h] = [e.alloc_register(f"bk{h}_{i}") for i in range(4)]
                        e.load(regs[h], rowt[0][0:1, k:k + 4])
                        regs["v"] = [e.snap(r_, min_val=0, max_val=AW * (NBK - 1)) for r_ in regs[h]]
                    q.plain(V, ld, *ready)
                accf = ACC[:, :, :].rearrange("p b w -> p (b w)")

                def fn(e, k=k):
                    o = accf[:, bass.ds(regs["v"][k % 4], width)]
                    return e.tensor_tensor(o, o, banks[k % na][:, 0:width], ALU.add)
                adds.append(op(V, fn, mm_[k], *adds[-1:]))
                hist["added"] = adds[-1]
            rowt = [row]
            if "src" in hist:
                rowt = [rowS]
            idx_, dlo_ = (idxS, dloS) if "src" in hist else (idx, dlo)

            def onehot(k):
                mf = [mm_[k - NM]] if k >= NM else hist["mfree"]
                if weighted:
                    fn = lambda e, k=k: e.tensor_scalar(M[k % NM][:, :], iot[:, :], dlo_[:, k:k + 1], wD[:, k:k + 1],
                                                        ALU.is_equal, ALU.mult)
                else:
                    fn = lambda e, k=k: e.tensor_scalar(M[k % NM][:, :], iot[:, :], dlo_[:, k:k + 1], None, ALU.is_equal)
                ms.append(op(V, fn, *mf, *ready))
            onehot(0)
            for k in range(chunks):
                gf = [mm_[k - NG]] if k >= NG else hist["gfree"]
                gs.append(dma(G_, lambda e, k=k: e.indirect_dma_start(
                    G[k % NG][:, 0:D], None, table, bass.IndirectOffsetOnAxis(ap=idx_[:, k:k + 1], axis=0)),
                    s_g[k % NG], *gf, *ready))
                if k + 1 < chunks:
                    onehot(k + 1)
                af = [adds[k - na]] if k >= na else hist["afree"]
                wc = [op(S, lambda e, k=k: e.copy(G[k % NG][:, D:D + 1], wD[:, k:k + 1]), *gf, *ready)] if width > D else []
                mm_.append(op(T, lambda e, k=k: e.matmul(banks[k % na][:, 0:width], M[k % NM][:, :], G[k % NG][:, 0:width],
                                                         start=True, stop=True), gs[k], ms[k], *wc, *af))
                credit += share
                while background is not None and credit > 0:
                    cost = next(background, None)
                    if cost is None:
                        background = None
                    else:
                        credit -= cost
                if k >= 1:
                    add(k - 1)
                    if need is not None and k >= PER_BLOCK * (need + 1) + SLACK:
                        need = next(units, None)
            add(chunks - 1)
            assert background is None
            hist["gfree"], hist["mfree"] = [mm_[-1]], [mm_[-1]]
            hist["afree"] = [adds[-1]] + hist.pop("bank", [])
            while need is not None:
                need = next(units, None)

        def layer(flagAP, ok, end, background=None, **kw):
            first_load = ndma[0]

            def version(chunks):
                ndma[0] = first_load
                units = end()
                bg = background() if background is not None else None
                if chunks == NCH:
                    aggregate(chunks=NCH, background=bg, **kw)
                    finish(units)
                else:
                    aggregate(chunks=NCF, background=bg, units=units, **kw)
                if held:
                    multiply()
            q.either(flagAP, [lambda: version(NCH), lambda: version(NCF)], [use, hist, rS, tabs], ok)
            npass[0] += 1

        tabs = {}

        def table_from(scale, TAB, Wt, wtok, stok, both=True, stage=False):
            tabs["toks"] = toks = []

            def make(b, tok, src=None):
                src = X[:, b, :] if src is None else src
                dst = G[b % NG][:, 0:D] if stage else ACC[:, b, 0:D]

                def evac(ph, mt):
                    w_ = [mt, stok(b)] + ([toks[b - NG]] if stage and b >= NG else [])
                    if stage or b % 2 and both:
                        t = op(S, lambda e: e.activation(dst, ph[:, 0:D], ACT.Copy, scale=scale[:, b:b + 1]), *w_)
                    else:
                        t = op(V, lambda e: e.tensor_scalar(dst, ph[:, 0:D], scale[:, b:b + 1], None, ALU.mult), *w_)
                    r = rows_of(b)
                    toks.append(dma("sync", lambda e: e.dma_start(TAB[1 + b * P:1 + b * P + r, :], dst[0:r, :]),
                                    by_name(f"s_sg{b % NG}") if stage else s_st[b % 2], t))
                    return t
                return project(src, Wt, D, [tok, *wtok], evac)
            return make

        then = table_from(d1, T1, W1, l_w, lambda b: k1, stage=True)
        for f in softmax(0):
            f()
        finish(transition(mix + [spread], then, before=(softmax, lambda g: GROUPS[g - 1] if g else -1)))
        multiply()
        toks = tabs["toks"]
        for i in range(2):
            for j in range(2):
                t = op(T, lambda e, i=i, j=j: e.transpose(PT[i][:, j * P:(j + 1) * P], W4r[:, j, i * P:(i + 1) * P],
                                                          ident[:, :]), *l_w, *use["pt"][-2:])
            wt = op(S, lambda e, i=i: e.copy(W4[:, i, 0:D], PT[i][:, 0:D]), t)
        use["pt"][-2:] = [wt, wt]
        o2 = fb.op
        alld = [*toks[-NG:], cps[-1], fl, k1]
        hk2 = split(keyi[0], [], [], op=o2)
        rF = {"base": rD["base"], "free": []}
        pay = scr[:, 0:2 * EC].rearrange("p (c o) -> p c o", o=2)
        adr = scr[:, 2 * EC:3 * EC].bitcast(I32)
        zf = o2(V, lambda e: e.memset(scr[:, 0:2 * NCH], 0.0))
        zd = load(SLOTD.rearrange("(p k) o -> p (k o)", p=P), scr[:, 0:2 * NCH], zf, queue=fb)
        finish(slots(rF, op=o2, after=hk2))
        o2(V, lambda e: e.tensor_copy(pay[:, :, 1], we[:, :]), zd, *l_we)
        v = o2(V, lambda e: e.tensor_copy(ti[:, :], rk[:, 0:EC]), rF["slots"])
        v = o2(V, lambda e: e.tensor_scalar(tj[:, :], ti[:, :], 127, None, ALU.bitwise_and), v)
        v = o2(V, lambda e: e.tensor_scalar(adr, ti[:, :], 7, None, ALU.logical_shift_right), v)
        v = o2(V, lambda e: e.scalar_tensor_tensor(out=ti[:, :], in0=tj[:, :], scalar=float(NCH), in1=adr,
                                                   op0=ALU.mult, op1=ALU.add), v)
        aD = o2(V, lambda e: e.tensor_copy(adr, ti[:, :]), v)
        v = o2(V, lambda e: e.tensor_scalar(rk[:, 0:EC], keyi[1][:, :], 1.0, 128.0, ALU.add, ALU.mult), aD, *l_src)
        pD = o2(V, lambda e: e.tensor_tensor(pay[:, :, 0], rk[:, 0:EC], lof[:, :], ALU.add), v)
        for c in range(EC):
            sD = fb.dma(G_, lambda e, c=c: e.indirect_dma_start(
                SLOTD, bass.IndirectOffsetOnAxis(ap=adr[:, c:c + 1].bitcast(U32), axis=0), pay[:, c, :], None,
                bounds_check=P * NCH - 1, oob_is_err=False), s_sD, aD, pD)
        l1 = load(scr[:, 0:2 * NCH], SLOTD.rearrange("(p k) o -> p (k o)", p=P), sD, queue=fb)
        slv = scr[:, 0:2 * NCH].rearrange("p (k o) -> p k o", o=2)
        idxi = idx[:, 0:NCH].bitcast(I32)
        v = o2(V, lambda e: e.tensor_copy(wD[:, 0:NCH], slv[:, :, 1]), l1)
        v = o2(V, lambda e: e.tensor_copy(idxi, slv[:, :, 0]))
        v = o2(V, lambda e: e.tensor_scalar(dlo[:, 0:NCH].bitcast(I32), idxi, 127, None, ALU.bitwise_and), v)
        v = o2(V, lambda e: e.tensor_copy(dlo[:, 0:NCH], dlo[:, 0:NCH].bitcast(I32)), v)
        v = o2(V, lambda e: e.tensor_scalar(idxi, idxi, 7, None, ALU.logical_shift_right), v)
        fb.plain(V, lambda e: None, v)
        q.branch((V, G_, "sync"), fb, flag[0:1, 0:1], *alld)
        joined = op(V, lambda e: e.memset(vpe[:, :], 0.0), *toks[-1:])
        l_row = [load(row[:, :], BKD[:, :], bkl)]
        rS = {}

        def by_src():
            w_ = [joined]
            hs = split(keyi[1], l_src, w_)
            yield 2.0
            bank = [PA[3][:, i * 64:(i + 1) * 64] for i in range(3)]
            yield from chunk_map(rS, bank[:2], hs, w_, okS)
            rS["bk"] = load(BKS.rearrange("o (p t) -> (o p) t", t=7), bki[:, :], rS["bki"])
            yield from slots(rS)
            A_, B_, L_, K_ = (scr[:, i * 832:i * 832 + EC] for i in range(4))
            yield 0.55
            f = op(V, lambda e: e.tensor_scalar(sc[0][:, 0:EC], keyi[0][:, :], 1.0, 128.0, ALU.add, ALU.mult), rS["slots"])
            yield 0.55
            f = op(V, lambda e: e.tensor_tensor(A_, sc[0][:, 0:EC], lof[:, :], ALU.add), f)
            yield 0.55
            f = op(V, lambda e: e.tensor_copy(ti, A_), f)
            yield 0.55
            f = op(V, lambda e: e.tensor_scalar(tj, ti, 1023, None, ALU.bitwise_and), f)
            yield 0.55
            f = op(V, lambda e: e.tensor_copy(B_, tj), f)
            yield 0.55
            f = op(V, lambda e: e.tensor_scalar(tj, ti, 10, None, ALU.logical_shift_right), f)
            yield 0.55
            f = op(V, lambda e: e.tensor_copy(A_, tj), f)
            yield 0.55
            f = op(V, lambda e: e.tensor_copy(ti, rk[:, 0:EC]), f)
            yield 0.55
            f = op(V, lambda e: e.tensor_scalar(tj, ti, 127, None, ALU.bitwise_and), f)
            yield 0.55
            f = op(V, lambda e: e.tensor_copy(L_, tj), f)
            yield 0.55
            f = op(V, lambda e: e.tensor_scalar(tj, ti, 7, None, ALU.logical_shift_right), f)
            rS["pay"] = op(V, lambda e: e.tensor_copy(K_, tj), f)
            yield from degrees(rS, bank[2], [rS["base"], *hs])
            v = op(V, lambda e: e.tensor_scalar(degS[:, :], bank[2][:, 0:NBK], 1.0, None, ALU.add), rS["deg"])
            hist["bank"] = [v]
            rS["k3"] = rsqrt_all(d3, degS[:, :], v, rqs)

        dg = {}

        def degree(g):
            sg = slice(GROUPS[g], GROUPS[g + 1])
            h = {}

            def start():
                h["t"] = op(V, lambda e: e.tensor_scalar(degI[:, sg], ACC[:, sg, D], 1.0, None, ALU.add), hist["added"])

            def mask():
                h["t"] = op(V, lambda e: e.tensor_scalar(dk[:, sg], degI[:, sg], 0.0, None, ALU.is_gt), h["t"])

            def floor():
                h["t"] = op(V, lambda e: e.tensor_scalar(degI[:, sg], degI[:, sg], 1e-30, None, ALU.max), h["t"])
                h["parts"] = rsqrt(d2, degI[:, sg], sg, h["t"])

            def part():
                h["t"] = h["parts"](h["t"])

            def masked():
                dg[g] = op(V, lambda e: e.tensor_tensor(d2[:, sg], d2[:, sg], dk[:, sg], ALU.mult), h["t"])
            return [start, mask, floor, part, part, part, part, masked]

        def add_scaled(scale):
            return lambda b, tok: op(V, lambda e: e.scalar_tensor_tensor(
                out=X[:, b, :], in0=ACC[:, b, 0:D], scalar=scale[:, b:b + 1], in1=X[:, b, :],
                op0=ALU.mult, op1=ALU.add), hist["added"])

        def end1():
            then = table_from(d2, T2, W2, l_w, lambda b: dg[GROUP_OF[b]])
            yield from transition([add_scaled(d1)], then, before=(degree, lambda g: GROUPS[g + 1] - 1))

        ready1 = [*toks[-NG:], *z_rows, *l_row, joined, zeroed[0]]
        hist["gfree"], hist["afree"] = toks[-NG:], [*cps, k1]
        layer(okD[0:1, 0:1], rD["ok"], end1, by_src, table=T1, weighted=False, ready=ready1, banks=PA[0:3], width=D + 1,
              share=0.43)

        def permute(piece, out_):
            pv = scr[:, piece * 832:piece * 832 + EC]
            npv = rk[:, 0:EC]
            rS["n"] = op(V, lambda e: e.tensor_scalar(npv, pv, -1.0, None, ALU.mult), rS["pay"], rS.get("p0", rS["pay"]))
            L_, K_ = (scr[:, i * 832:i * 832 + EC] for i in (2, 3))
            oh = [big[i][:, 0:NCH] for i in range(3)]
            ol = [big[i][:, NCH:NCH + P] for i in range(3)]
            ab = M2
            rd, rl, mms = [], [], []
            w0 = [*hist["afree"], rS["pay"], rS["deg"], c_iok, rS["n"]]

            def products(c):
                op(T, lambda e: e.matmul(PA[2][:, 0:512], ol[c % 3], oh[c % 3][:, 0:512], start=c == 0, stop=c == EC - 1),
                   rd[c], rl[c])
                mms.append(op(T, lambda e: e.matmul(PA[3][:, 0:NCH - 512], ol[c % 3], oh[c % 3][:, 512:NCH],
                                                    start=c == 0, stop=c == EC - 1)))
            for c in range(EC):
                free = [mms[c - 3]] if c >= 3 else w0
                rd.append(op(V, lambda e, c=c: e.tensor_scalar(oh[c % 3], iok[:, 0:NCH], K_[:, c:c + 1], None,
                                                               ALU.is_equal), *free))
                v = op(S, lambda e, c=c: e.activation(ab[c % 2][:, :], iot[:, :], ACT.Abs, bias=L_[:, c:c + 1], scale=-1.0),
                       *(w0 if c < 2 else [rl[c - 2]]))
                rl.append(op(S, lambda e, c=c: e.activation(ol[c % 3], ab[c % 2][:, :], ACT.Relu, bias=pv[:, c:c + 1],
                                                            scale=npv[:, c:c + 1]), v, *free))
                if c >= 1:
                    products(c - 1)
                yield 1.0
            products(EC - 1)
            e1 = op(S, lambda e: e.copy(out_[:, 0:512], PA[2][:, 0:512]), mms[-1])
            e1 = op(S, lambda e: e.copy(out_[:, 512:NCH], PA[3][:, 0:NCH - 512]))
            rS[f"p{piece}"] = e1
            hist["bank"] = [e1]

        halves = PA[0:2]

        def end2():
            then = table_from(d2, T3, W3, l_w, lambda b: k1, both=False)
            tr, hv = [], {}

            def hidden(b):
                h_ = hb[b % 3]
                v = op(V, lambda e: e.scalar_tensor_tensor(out=h_[:, :], in0=ACC[:, b, 0:D], scalar=d2[:, b:b + 1],
                                                           in1=b1[:, :], op0=ALU.mult, op1=ALU.add),
                       hist["added"], *l_b, *([tr[b - 3]] if b >= 3 else []))
                hv[b] = op(S, lambda e: e.activation(h_[:, :], h_[:, :], ACT.Relu), v)
            for b in range(NBK + 2):
                if b < NBK:
                    yield b
                    hidden(b)
                if b >= 2:
                    yield min(b, NBK - 1)
                    tr.append(then(b - 2, hv[b - 2], hb[(b - 2) % 3][:, :]))

        layer(okD[0:1, 0:1], rD["ok"], end2, lambda: permute(0, sc[0]), table=T2, weighted=True,
              ready=tabs["toks"][-2:], banks=halves, share=1.0)

        idxS, dloS = scr[:, 0:NCH].bitcast(U32), scr[:, NCH:2 * NCH]
        rowS = scr[0:1, 2 * NCH:3 * NCH].bitcast(I32)

        def contents():
            yield from permute(1, sc[1])
            w_ = [rS["p0"], rS["p1"]]
            v = op(V, lambda e: e.scalar_tensor_tensor(out=rk[:, 0:NCH], in0=sc[0][:, 0:NCH], scalar=1024.0,
                                                       in1=sc[1][:, 0:NCH], op0=ALU.mult, op1=ALU.add), *w_)
            yield 1.0
            idxs, dlos = idxS.bitcast(I32), dloS.bitcast(I32)
            v = op(V, lambda e: e.tensor_copy(idxs, rk[:, 0:NCH]), v)
            yield 1.0
            v1 = op(V, lambda e: e.tensor_scalar(dlos, idxs, 127, None, ALU.bitwise_and), v)
            yield 1.0
            v2 = op(V, lambda e: e.tensor_copy(dloS, dlos), v1)
            yield 1.0
            v3_ = op(V, lambda e: e.tensor_scalar(idxs, idxs, 7, None, ALU.logical_shift_right), v1)
            rS["src"] = [v2, v3_, load(rowS, BKS[0:1, 0:NCH], rS["bk"], *w_)]
            yield 1.0

        def biased(b, tok):
            return op(V, lambda e: e.scalar_tensor_tensor(out=hb[b % 3][:, :], in0=ACC[:, b, 0:D], scalar=d2[:, b:b + 1],
                                                          in1=b2[:, :], op0=ALU.mult, op1=ALU.add), hist["added"],
                      *([use["br"][b - 3]] if b >= 3 else [*use["tr"][-1:]]))

        def add_relu(b, tok):
            t = op(V, lambda e: e.scalar_tensor_tensor(
                out=X[:, b, :], in0=hb[b % 3][:, :], scalar=0.0, in1=X[:, b, :], op0=ALU.max, op1=ALU.add), tok)
            use["br"].append(t)
            return t

        def end3():
            use["br"] = []
            then = table_from(d3, T4, W4, [wt], lambda b: rS["k3"])
            yield from transition([biased, add_relu], then)

        layer(okD[0:1, 0:1], rD["ok"], end3, contents, table=T3, weighted=True,
              ready=tabs["toks"][-2:], banks=halves, share=1.0)

        def store(b, tok):
            r = rows_of(b)
            dma("sync", lambda e: e.dma_start(out[b * P:b * P + r, :], X[0:r, b, :]), s_out, tok)
        hist["src"] = True
        layer(okS[0:1, 0:1], rS["ok"], lambda: transition([add_scaled(d3)], store), table=T4, weighted=False,
              ready=[*tabs["toks"][-2:], *rS["src"]], banks=halves)
        q.plain("sync", lambda e: e.wait_ge(s_out, q.dma_n[s_out]), *l_we, *l_src, *l_pad)

        block = ctx.enter_context(nc.Block())
        block.sync(lambda e: q.run("sync", e))
        block.vector(lambda e: q.run("vector", e))
        block.scalar(lambda e: q.run("scalar", e))
        block.tensor(lambda e: q.run("tensor", e))
        block.gpsimd(lambda e: q.run("gpsimd", e))


def kernel(**inputs):
    import numpy as np
    import concourse.bacc as bacc
    from concourse.bass_utils import run_bass_kernel_spmd as run
    nc = bacc.Bacc("TRN2", target_bir_lowering=False, num_devices=1)
    arrays, args = {}, {}
    for name, v in inputs.items():
        v = np.ascontiguousarray(v)
        arrays[f"in_{name}"] = v
        args[name] = nc.dram_tensor(f"in_{name}", v.shape, mybir.dt.from_np(v.dtype), kind="ExternalInput").ap()
    out = nc.dram_tensor("out_0", (N, D), F32, kind="ExternalOutput").ap()
    program(nc, args, out)
    r = run(nc, [arrays], core_ids=[0])
    return r.results[0]["out_0"]
```
